# Optimizing a Trainium2 kernel written in Bass

```python
import numpy as np
import jax
import jax.numpy as jnp

def _softmax(x, axis=-1):
    return jax.nn.softmax(x, axis=axis)

def _gelu(x):
    return jax.nn.gelu(x, approximate=True)

def _silu(x):
    return jax.nn.silu(x)

def _sigmoid(x):
    return jax.nn.sigmoid(x)

def _layernorm(x, axis=-1, eps=1e-05):
    m = jnp.mean(x, axis=axis, keepdims=True)
    v = jnp.var(x, axis=axis, keepdims=True)
    return (x - m) / jnp.sqrt(v + eps)

def _scatter_add(tgt, idx, src, axis=0):
    return tgt.at[idx].add(src)

def _segment_sum(src, seg, n):
    return jax.ops.segment_sum(src, seg, n)
kernel_name = 'mk_vit_tower_d1_tok_img512_r4_4118a8'

def setup_inputs(seed: int=0):
    np.random.seed(seed)
    _w = jnp.asarray

    def _rec_inputs():
        import jax
        import jax.numpy as jnp
        _rk = jax.random.key(seed)
        x = -0.000178447 + 0.99995 * jax.random.normal(jax.random.fold_in(_rk, 1), (64, 3, 176, 208), jnp.float32)
        return x
    x = _rec_inputs()

    def _L0_tok_setup():
        import jax, jax.numpy as jnp
        import numpy as np
        P1, P2, C = (16, 16, 3)
        PW, PH = (176 // P1, 208 // P2)
        key = jax.random.key(seed)
        k1, k2, k3, k4, k5 = jax.random.split(key, 5)
        B, D = (64, 128)
        patch_dim = P1 * P2 * C
        return {'x': jax.random.normal(k1, (B, C, PW * P1, PH * P2), dtype=jnp.float32), 'W': jax.random.normal(k2, (D, patch_dim), dtype=jnp.float32) * 0.02, 'b': jax.random.normal(k3, (D,), dtype=jnp.float32) * 0.02, 'cls_token': jax.random.uniform(k4, (1, 1, D), dtype=jnp.float32), 'pos_emb': jax.random.normal(k5, (1, PW * PH + 1, 1), dtype=jnp.float32)}
    _L0_tok_all = _L0_tok_setup()
    _L0_tok_in = {k: v for k, v in _L0_tok_all.items() if k in ('W', 'b', 'cls_token', 'pos_emb')}
    del _L0_tok_all

    def _L0_attn_setup():
        import jax, jax.numpy as jnp
        import numpy as np
        import math
        B, L, DIM, H = (2, 512, 128, 8)
        key = jax.random.key(seed)
        ks = jax.random.split(key, 8)
        s = 0.02
        return {'x': jax.random.normal(ks[0], (B, L, DIM), dtype=jnp.float32), 'Wq': jax.random.normal(ks[1], (DIM, DIM), dtype=jnp.float32) * s, 'Wk': jax.random.normal(ks[2], (DIM, DIM), dtype=jnp.float32) * s, 'Wv': jax.random.normal(ks[3], (DIM, DIM), dtype=jnp.float32) * s, 'Wb': jax.random.normal(ks[4], (H, DIM), dtype=jnp.float32) * s, 'mixing': jax.random.normal(ks[5], (H, DIM), dtype=jnp.float32) * 0.2, 'Wd': jax.random.normal(ks[6], (DIM, DIM), dtype=jnp.float32) * s, 'bd': jax.random.normal(ks[7], (DIM,), dtype=jnp.float32) * s}
    _L0_attn_all = _L0_attn_setup()
    _L0_attn_in = {k: v for k, v in _L0_attn_all.items() if k in ('Wq', 'Wk', 'Wv', 'Wb', 'mixing', 'Wd', 'bd')}
    del _L0_attn_all

    def _L0_ffn_setup():
        import jax, jax.numpy as jnp
        import numpy as np
        D_MODEL = 128
        D_FF = 128
        N_EXPERTS = 16
        TOP_K = 3
        BATCH, SEQ = (1, 512)

        def _swiglu(combined):
            gate, up = jnp.split(combined, 2, axis=-1)
            return jax.nn.silu(gate) * up
        key = jax.random.key(seed)
        ks = jax.random.split(key, 6)
        x = jax.random.normal(ks[0], (BATCH, SEQ, D_MODEL), dtype=jnp.float32)
        gate_w = 0.01 * jax.random.normal(ks[1], (N_EXPERTS, D_MODEL), dtype=jnp.float32)
        expert_bias = jnp.zeros((N_EXPERTS,), dtype=jnp.float32)
        shared_gate_up = 0.02 * jax.random.normal(ks[2], (2 * D_FF, D_MODEL), dtype=jnp.float32)
        shared_down = 0.02 * jax.random.normal(ks[3], (D_MODEL, D_FF), dtype=jnp.float32)
        expert_gate_up = 0.02 * jax.random.normal(ks[4], (N_EXPERTS, 2 * D_FF, D_MODEL), dtype=jnp.float32)
        expert_down = 0.02 * jax.random.normal(ks[5], (N_EXPERTS, D_MODEL, D_FF), dtype=jnp.float32)
        return {'x': x, 'gate_w': gate_w, 'expert_bias': expert_bias, 'shared_gate_up': shared_gate_up, 'shared_down': shared_down, 'expert_gate_up': expert_gate_up, 'expert_down': expert_down}
    _L0_ffn_all = _L0_ffn_setup()
    _L0_ffn_in = {k: v for k, v in _L0_ffn_all.items() if k in ('gate_w', 'expert_bias', 'shared_gate_up', 'shared_down', 'expert_gate_up', 'expert_down')}
    del _L0_ffn_all
    return {'x': x, 'L0_tok_W': _L0_tok_in['W'], 'L0_tok_b': _L0_tok_in['b'], 'L0_tok_cls_token': _L0_tok_in['cls_token'], 'L0_tok_pos_emb': _L0_tok_in['pos_emb'], 'L0_attn_Wq': _L0_attn_in['Wq'], 'L0_attn_Wk': _L0_attn_in['Wk'], 'L0_attn_Wv': _L0_attn_in['Wv'], 'L0_attn_Wb': _L0_attn_in['Wb'], 'L0_attn_mixing': _L0_attn_in['mixing'], 'L0_attn_Wd': _L0_attn_in['Wd'], 'L0_attn_bd': _L0_attn_in['bd'], 'L0_ffn_gate_w': _L0_ffn_in['gate_w'], 'L0_ffn_expert_bias': _L0_ffn_in['expert_bias'], 'L0_ffn_shared_gate_up': _L0_ffn_in['shared_gate_up'], 'L0_ffn_shared_down': _L0_ffn_in['shared_down'], 'L0_ffn_expert_gate_up': _L0_ffn_in['expert_gate_up'], 'L0_ffn_expert_down': _L0_ffn_in['expert_down']}

def reference(x, L0_tok_W, L0_tok_b, L0_tok_cls_token, L0_tok_pos_emb, L0_attn_Wq, L0_attn_Wk, L0_attn_Wv, L0_attn_Wb, L0_attn_mixing, L0_attn_Wd, L0_attn_bd, L0_ffn_gate_w, L0_ffn_expert_bias, L0_ffn_shared_gate_up, L0_ffn_shared_down, L0_ffn_expert_gate_up, L0_ffn_expert_down):
    import jax
    import jax.numpy as jnp

    def _L0_tok_ref(x, W, b, cls_token, pos_emb):
        import jax, jax.numpy as jnp
        import numpy as np
        P1, P2, C = (16, 16, 3)
        PW, PH = (176 // P1, 208 // P2)
        B = x.shape[0]
        patches = x.reshape(B, C, PW, P1, PH, P2)
        patches = patches.transpose(0, 2, 4, 3, 5, 1).reshape(B, PW * PH, P1 * P2 * C)
        proj = jnp.einsum('bnp,dp->bnd', patches, W) + b
        cls = jnp.broadcast_to(cls_token, (B, 1, cls_token.shape[-1]))
        out = jnp.concatenate([cls, proj], axis=1) + pos_emb
        return out

    def _L0_attn_ref(x, Wq, Wk, Wv, Wb, mixing, Wd, bd):
        import jax, jax.numpy as jnp
        import numpy as np
        import math
        B, L, DIM, H = (2, 512, 128, 8)
        b, l, d = x.shape
        h = mixing.shape[0]
        dh = d // h
        q = x @ Wq.T
        k = x @ Wk.T
        v = (x @ Wv.T).reshape(b, l, h, dh).transpose(0, 2, 1, 3)
        scores = jnp.einsum('bld,hd,bsd->bhls', q, mixing, k)
        cb = jnp.einsum('bsd,hd->bhs', x, Wb)
        scale = math.sqrt(d / h)
        scores = (scores + cb[:, :, None, :]) / scale
        probs = jax.nn.softmax(scores, axis=-1)
        ctx = jnp.einsum('bhls,bhsd->bhld', probs, v)
        ctx = ctx.transpose(0, 2, 1, 3).reshape(b, l, d)
        return ctx @ Wd.T + bd

    def _L0_ffn_ref(x, gate_w, expert_bias, shared_gate_up, shared_down, expert_gate_up, expert_down):
        import jax, jax.numpy as jnp
        import numpy as np
        D_MODEL = 128
        D_FF = 128
        N_EXPERTS = 16
        TOP_K = 3
        BATCH, SEQ = (1, 512)

        def _swiglu(combined):
            gate, up = jnp.split(combined, 2, axis=-1)
            return jax.nn.silu(gate) * up
        B, S, D = x.shape
        xf = x.reshape(-1, D)
        shared_out = _swiglu(xf @ shared_gate_up.T) @ shared_down.T
        logits = xf @ gate_w.T
        affinity = jax.nn.sigmoid(logits)
        routing_scores = affinity + expert_bias
        _, sel = jax.lax.top_k(routing_scores, TOP_K)
        sel_aff = jnp.take_along_axis(affinity, sel, axis=1)
        gating = sel_aff / (sel_aff.sum(axis=-1, keepdims=True) + 1e-09)
        combined = jnp.einsum('td,efd->tef', xf, expert_gate_up)
        hidden = _swiglu(combined)
        expert_out = jnp.einsum('tef,edf->ted', hidden, expert_down)
        sel_out = jnp.take_along_axis(expert_out, sel[:, :, None], axis=1)
        routed_out = jnp.einsum('tk,tkd->td', gating, sel_out)
        out = shared_out + routed_out
        return out.reshape(B, S, D)
    h = _L0_tok_ref(x, L0_tok_W, L0_tok_b, L0_tok_cls_token, L0_tok_pos_emb)
    h = h + _L0_attn_ref(_layernorm(h, axis=-1), L0_attn_Wq, L0_attn_Wk, L0_attn_Wv, L0_attn_Wb, L0_attn_mixing, L0_attn_Wd, L0_attn_bd)
    h = h + _L0_ffn_ref(_layernorm(h, axis=-1), L0_ffn_gate_w, L0_ffn_expert_bias, L0_ffn_shared_gate_up, L0_ffn_shared_down, L0_ffn_expert_gate_up, L0_ffn_expert_down)
    return h

_drawn_inputs = setup_inputs


def setup_inputs(seed=0):
    import zlib

    import numpy as np

    out = dict(_drawn_inputs(seed))
    spreads = {'L0_ffn_expert_bias': (0.0, 0.8)}
    factors = {'L0_tok_b': 3.199,
     'L0_tok_cls_token': 2.744,
     'L0_attn_Wq': 8.0,
     'L0_attn_Wk': 8.0,
     'L0_attn_Wv': 8.0,
     'L0_attn_Wb': 8.0,
     'L0_attn_mixing': 8.0,
     'L0_attn_Wd': 8.0,
     'L0_attn_bd': 3.052,
     'L0_ffn_gate_w': 8.0,
     'L0_ffn_shared_gate_up': 8.0,
     'L0_ffn_shared_down': 8.0,
     'L0_ffn_expert_gate_up': 8.0,
     'L0_ffn_expert_down': 8.0}
    for name, (base, spread) in spreads.items():
        noise = np.random.default_rng([zlib.crc32(name.encode()), seed]).standard_normal(out[name].shape)
        drawn = base * np.exp(spread * noise) if base else spread * noise
        out[name] = jnp.asarray(drawn.astype(out[name].dtype))
    for name, factor in factors.items():
        out[name] = (out[name] * factor).astype(out[name].dtype)
    return out
```

```python
from contextlib import ExitStack

import concourse.bass as bass
from concourse import mybir

F32 = mybir.dt.float32
F32R = mybir.dt.float32r
ALU = mybir.AluOpType
ACT = mybir.ActivationFunctionType
AX = mybir.AxisListType

D = 128
B = 64
NP = 143
L = NP + 1
T = B * L
PK = 6
IMG_LOAD = 4
H = 8
DH = D // H
PAIR = 2 * L
PAIRS = B // 2
HL = H * L
QT = HL // 128
SC = L // 2
TC = 512
TILES = T // TC
E = 16
NE = E + 1
TOPK = 3
EPS = 1e-5
LOWEST = -3.0e38
GC = 4


def after(eng, sem, n):
    if not isinstance(n, int) or n > 0:
        eng.wait_ge(sem, n)


def norm_stage(nc, name, resid, xn, mean_w, eps):
    N = 3
    with ExitStack() as ctx:
        cen = ctx.enter_context(nc.sbuf_tensor(f"{name}_cen", [D, N, TC], F32))
        sq = ctx.enter_context(nc.sbuf_tensor(f"{name}_sq", [D, N, TC], F32))
        std = ctx.enter_context(nc.sbuf_tensor(f"{name}_std", [D, N, TC], F32))
        mean_ps = ctx.enter_context(nc.psum_tensor(f"{name}_mean_ps", [D, N, TC], F32))
        var_ps = ctx.enter_context(nc.psum_tensor(f"{name}_var_ps", [D, N, TC], F32))
        mean_ready = ctx.enter_context(nc.semaphore(f"{name}_mean_ready"))
        centred = ctx.enter_context(nc.semaphore(f"{name}_centred"))
        squared = ctx.enter_context(nc.semaphore(f"{name}_squared"))
        var_ready = ctx.enter_context(nc.semaphore(f"{name}_var_ready"))
        std_ready = ctx.enter_context(nc.semaphore(f"{name}_std_ready"))
        inv_ready = ctx.enter_context(nc.semaphore(f"{name}_inv_ready"))
        normed = ctx.enter_context(nc.semaphore(f"{name}_normed"))
        block = ctx.enter_context(nc.Block())

        @block.tensor
        def _(pe):
            def step(i):
                for k in range(N):
                    after(pe, centred, (i - 1) * N + k + 1)
                    pe.matmul(mean_ps[:, k, :], mean_w[:, :], resid[:, bass.ds(i * (N * TC) + k * TC, TC)],
                              start=True, stop=True).then_inc(mean_ready, 1)
                for k in range(N):
                    pe.wait_ge(squared, i * N + k + 1)
                    after(pe, std_ready, (i - 1) * N + k + 1)
                    pe.matmul(var_ps[:, k, :], mean_w[:, :], sq[:, k, :],
                              start=True, stop=True).then_inc(var_ready, 1)

            step(0)
            with pe.Fori(1, TILES // N) as i:
                step(i)

        @block.scalar
        def _(act):
            def step(i):
                for k in range(N):
                    act.wait_ge(centred, i * N + k + 1)
                    after(act, var_ready, (i - 1) * N + k + 1)
                    act.activation(sq[:, k, :], cen[:, k, :], ACT.Square).then_inc(squared, 1)
                for k in range(N):
                    act.wait_ge(var_ready, i * N + k + 1)
                    after(act, normed, (i - 1) * N + k + 1)
                    act.activation(std[:, k, :], var_ps[:, k, :], ACT.Sqrt, bias=eps[:, 0:1]).then_inc(std_ready, 1)

            step(0)
            with act.Fori(1, TILES // N) as i:
                step(i)

        @block.vector
        def _(dve):
            def step(i):
                for k in range(N):
                    dve.wait_ge(mean_ready, i * N + k + 1)
                    after(dve, normed, (i - 1) * N + k + 1)
                    dve.tensor_tensor(cen[:, k, :], resid[:, bass.ds(i * (N * TC) + k * TC, TC)],
                                      mean_ps[:, k, :], ALU.subtract).then_inc(centred, 1)
                for k in range(N):
                    dve.wait_ge(std_ready, i * N + k + 1)
                    dve.reciprocal(std[:, k, :], std[:, k, :]).then_inc(inv_ready, 1)
                for k in range(N):
                    dve.wait_ge(inv_ready, i * N + k + 1)
                    dve.tensor_tensor(xn[:, bass.ds(i * (N * TC) + k * TC, TC)], cen[:, k, :],
                                      std[:, k, :], ALU.mult).then_inc(normed, 1)

            step(0)
            with dve.Fori(1, TILES // N) as i:
                step(i)


def tower(nc, xp, w_tok, cols, pos, wq, wk, wv_t, wd_t, gate_t, ebias, egu_t, ed_t, ident, out):
    G4 = IMG_LOAD * NP
    outer = ExitStack()
    with outer:
        def sb(name, shape, dt=F32):
            return outer.enter_context(nc.sbuf_tensor(name, shape, dt))

        resid = sb("resid", [D, T])
        xn = sb("xn", [D, T])
        gu_hi = sb("gu_hi", [D, NE, 2 * D], F32R)
        gu_lo = sb("gu_lo", [D, NE, 2 * D], F32R)
        down = sb("down", [D, NE, D])
        b_hi = sb("b_hi", [D, H, D], F32R)
        b_lo = sb("b_lo", [D, H, D], F32R)
        mean_w = sb("mean_w", [D, D])
        eps = sb("eps", [D, 1])
        eye = sb("eye", [D, D])
        wv_sb = sb("wv_sb", [D, D])
        wd_sb = sb("wd_sb", [D, D])
        gw_sb = sb("gw_sb", [D, E])
        eb_sb = sb("eb_sb", [128, E])
        col_sb = sb("col_sb", [D, 3 + 2 * H])
        wb4 = sb("wb4", [D, H])
        gates_dram = nc.dram_tensor("gates_dram", (TILES, E, TC), F32, kind="Internal").ap()

        with ExitStack() as ctx:
            def sb2(name, shape, dt=F32):
                return ctx.enter_context(nc.sbuf_tensor(name, shape, dt))

            def sem(name):
                return ctx.enter_context(nc.semaphore(name))

            patches = sb2("patches", [128, 2, PK, G4])
            wt_sb = sb2("wt_sb", [128, PK, D])
            posb = sb2("posb", [D, L])
            gu_raw = sb2("gu_raw", [D, NE, 2 * D])
            wq_sb = sb2("wq_sb", [D, D])
            wk_sb = sb2("wk_sb", [D, D])
            wkm = sb2("wkm", [D, H, D])
            emb_ps = ctx.enter_context(nc.psum_tensor("emb_ps", [D, 4, 512], F32))
            b_ps = ctx.enter_context(nc.psum_tensor("b_ps", [D, 2, 512], F32))

            wt_in = sem("wt_in")
            attn_in = sem("attn_in")
            pos_in = sem("pos_in")
            gu_in = sem("gu_in")
            rest_in = sem("rest_in")
            load_in = [sem("load_in0"), sem("load_in1")]
            mm_done = sem("mm_done")
            posb_ready = sem("posb_ready")
            stored = sem("stored")
            wkm_ready = sem("wkm_ready")
            b_ready = sem("b_ready")
            b_high = sem("b_high")
            b_low = sem("b_low")
            gu_high = sem("gu_high")
            consts = sem("consts")
            block = ctx.enter_context(nc.Block())
            LOADS = B // IMG_LOAD

            @block.sync
            def _(sp):
                sp.dma_start(wt_sb[:, :, :], w_tok.rearrange("k p d -> p k d")).then_inc(wt_in, 16)
                sp.dma_start(col_sb[:, :], cols).then_inc(pos_in, 16)
                sp.dma_start(posb[:, :], pos.partition_broadcast(D)).then_inc(pos_in, 16)

                def load(i):
                    for s in range(2):
                        after(sp, mm_done, (i - 1) * 4 + 2 * s + 2)
                        sp.dma_start(patches[:, s, :, :],
                                     xp[bass.ds(i * 2 + s, 1)].rearrange("o p k n -> (o p) k n")).then_inc(load_in[s], 16)

                load(0)
                with sp.Fori(1, LOADS // 2) as i:
                    load(i)

            @block.scalar
            def _(act):
                act.dma_start(wq_sb[:, :], wq).then_inc(attn_in, 16)
                act.dma_start(wk_sb[:, :], wk).then_inc(attn_in, 16)
                act.dma_start(wv_sb[:, :], wv_t).then_inc(rest_in, 16)
                act.dma_start(wd_sb[:, :], wd_t).then_inc(rest_in, 16)
                act.dma_start(gw_sb[:, :], gate_t).then_inc(rest_in, 16)
                act.dma_start(eye[:, :], ident).then_inc(rest_in, 16)
                act.dma_start(eb_sb[:, :], ebias.partition_broadcast(128)).then_inc(rest_in, 16)
                act.dma_start(gu_raw[:, :, :], egu_t).then_inc(gu_in, 16)
                act.dma_start(down[:, :, :], ed_t).then_inc(rest_in, 16)
                for h in range(0, H, 4):
                    act.wait_ge(b_ready, h // 4 + 1)
                    act.activation(b_hi[:, h:h + 4, :], b_ps[:, h // 4, :].rearrange("p (a b) -> p a b", a=4),
                                   ACT.Copy).then_inc(b_high, 1)
                act.wait_ge(gu_in, 16)
                for e in range(NE):
                    act.activation(gu_hi[:, e, :], gu_raw[:, e, :], ACT.Copy).then_inc(gu_high, 1)
                act.wait_ge(rest_in, 16 * 6)

            @block.gpsimd
            def _(pool):
                pool.memset(mean_w[:, :], 1.0 / D)
                pool.memset(eps[:, :], EPS)
                for e in range(NE):
                    pool.wait_ge(gu_high, e + 1)
                    pool.tensor_tensor(gu_lo[:, e, :], gu_raw[:, e, :], gu_hi[:, e, :].bitcast(F32),
                                       ALU.subtract).then_inc(consts, 1)
                pool.wait_ge(consts, NE)

            @block.tensor
            def _(pe):
                for h in range(H):
                    pe.wait_ge(wkm_ready, h + 1)
                    mm = pe.matmul(b_ps[:, h // 4, bass.ts(h % 4, D)], wq_sb[:, :], wkm[:, h, :],
                                   start=True, stop=True, skip_group_check=True)
                    if h % 4 == 3:
                        mm.then_inc(b_ready, 1)
                pe.wait_ge(wt_in, 16)

                def step(i):
                    for s in range(2):
                        pe.wait_ge(load_in[s], i * 16 + 16)
                        for p in range(2):
                            after(pe, stored, (i - 1) * 4 + 2 * s + p + 1)
                            for k in range(PK):
                                mm = pe.matmul(emb_ps[:, 2 * s + p, 0:2 * NP], wt_sb[:, k, :],
                                               patches[:, s, k, bass.ts(p, 2 * NP)],
                                               start=(k == 0), stop=(k == PK - 1))
                            mm.then_inc(mm_done, 1)

                step(0)
                with pe.Fori(1, LOADS // 2) as i:
                    step(i)

            @block.vector
            def _(dve):
                dve.wait_ge(attn_in, 32)
                dve.wait_ge(pos_in, 32)
                for h in range(H):
                    dve.tensor_scalar(wkm[:, h, :], wk_sb[:, :], col_sb[:, 3 + h:4 + h], 0.25,
                                      ALU.mult, ALU.mult).then_inc(wkm_ready, 1)
                dve.tensor_scalar(wb4[:, :], col_sb[:, 3 + H:3 + 2 * H], 0.25, None, ALU.mult)
                dve.tensor_scalar(posb[:, 0:1], posb[:, 0:1], col_sb[:, 1:2], None, ALU.add).then_inc(posb_ready, 1)
                dve.tensor_scalar(posb[:, 1:L], posb[:, 1:L], col_sb[:, 0:1], None, ALU.add).then_inc(posb_ready, 1)
                for h in range(0, H, 4):
                    dve.wait_ge(b_high, h // 4 + 1)
                    dve.tensor_tensor(b_lo[:, h:h + 4, :], b_ps[:, h // 4, :].rearrange("p (a b) -> p a b", a=4),
                                      b_hi[:, h:h + 4, :].bitcast(F32), ALU.subtract).then_inc(b_low, 1)
                dve.wait_ge(posb_ready, 2)
                by_image = resid[:, :].rearrange("d (b l) -> d b l", l=L)
                dve.tensor_copy(by_image[:, :, 0], posb[:, 0:1].broadcast_to([D, B]))
                with dve.Fori(0, LOADS // 2) as i:
                    for s in range(2):
                        for p in range(2):
                            dve.wait_ge(mm_done, i * 4 + 2 * s + p + 1)
                            dve.tensor_tensor(
                                by_image[:, bass.ds(i * 8 + 4 * s + 2 * p, 2), 1:L],
                                emb_ps[:, 2 * s + p, 0:2 * NP].rearrange("d (b n) -> d b n", n=NP),
                                posb[:, 1:L].unsqueeze(1).broadcast_to([D, 2, NP]), ALU.add).then_inc(stored, 1)

        norm_stage(nc, "norm1", resid, xn, mean_w, eps)

        with ExitStack() as ctx:
            def sb3(name, shape, dt=F32):
                return ctx.enter_context(nc.sbuf_tensor(name, shape, dt))

            def sem(name):
                return ctx.enter_context(nc.semaphore(name))

            x_st = sb3("x_st", [D, PAIR])
            x_hi = sb3("x_hi", [D, PAIR], F32R)
            x_lo = sb3("x_lo", [D, PAIR], F32R)
            y = sb3("y", [D, 2, HL])
            v = sb3("v", [SC, 4, 2, D])
            probs = sb3("probs", [128, 2, QT, L])
            probs_t = sb3("probs_t", [SC, 2, 2, HL])
            neg_max = sb3("neg_max", [128, 2, QT])
            row_sum = sb3("row_sum", [128, 2, QT])
            inv_sum = sb3("inv_sum", [128, 2, QT])
            ctx_sb = sb3("ctx_sb", [D, PAIR])
            ps = ctx.enter_context(nc.psum_tensor("attn_ps", [128, 8, 512], F32))

            split_done = sem("split_done")
            v_ready = sem("v_ready")
            v_stored = sem("v_stored")
            y_ready = sem("y_ready")
            y_stored = sem("y_stored")
            scores_ready = sem("scores_ready")
            max_ready = sem("max_ready")
            exp_done = sem("exp_done")
            inv_ready = sem("inv_ready")
            probs_ready = sem("probs_ready")
            t_ready = sem("t_ready")
            t_stored_v = sem("t_stored_v")
            t_stored_s = sem("t_stored_s")
            ctx_ready = sem("ctx_ready")
            ctx_stored = sem("ctx_stored")
            o_ready = sem("o_ready")
            added = sem("added")
            v_zero = sem("v_zero")
            x_high = sem("x_high")
            block = ctx.enter_context(nc.Block())

            @block.gpsimd
            def _(pool):
                def low_part(i):
                    pool.wait_ge(x_high, i + 1)
                    pool.tensor_tensor(x_lo[:, :], x_st[:, :], x_hi[:, :].bitcast(F32),
                                       ALU.subtract).then_inc(split_done, 1)

                def normalise(i):
                    for m in range(2):
                        pool.wait_ge(inv_ready, i * 2 + m + 1)
                        pool.tensor_tensor(probs[:, m, :, :], probs[:, m, :, :],
                                           inv_sum[:, m, :].unsqueeze(2).broadcast_to([128, QT, L]),
                                           ALU.mult).then_inc(probs_ready, 1)

                low_part(0)
                with pool.Fori(0, PAIRS - 1) as i:
                    low_part(i + 1)
                    normalise(i)
                normalise(PAIRS - 1)

            @block.tensor
            def _(pe):
                def y_products(i, first):
                    pe.wait_ge(split_done, i + 1)
                    for h in range(H):
                        bank = 7 - h % 2
                        if h == 1 and not first:
                            pe.wait_ge(v_stored, i)
                        if h >= 2:
                            pe.wait_ge(y_stored, i * H + h - 1)
                        out_ = ps[:, bank, 0:PAIR]
                        pe.matmul(out_, b_hi[:, h, :], x_hi[:, :], start=True, stop=False)
                        pe.matmul(out_, b_hi[:, h, :], x_lo[:, :], start=False, stop=False)
                        pe.matmul(out_, b_lo[:, h, :], x_hi[:, :], start=False, stop=True).then_inc(y_ready, 1)

                def values(i):
                    pe.wait_ge(split_done, i + 1)
                    pe.wait_ge(y_stored, (i + 1) * H)
                    for q in range(4):
                        mm = pe.matmul(ps[0:SC, 6, bass.ts(q, D)], x_st[:, bass.ts(q, SC)], wv_sb[:, :],
                                       start=True, stop=True, skip_group_check=True)
                    mm.then_inc(v_ready, 1)

                def scores(i, m):
                    for t in range(QT):
                        if m == 0 and t == 6:
                            pe.wait_ge(added, i)
                        mm = pe.matmul(ps[:, 3 * m + t // 3, bass.ts(t % 3, L)], y[:, m, bass.ts(t, 128)],
                                       xn[:, bass.ds(i * PAIR + m * L, L)], start=True, stop=True,
                                       skip_group_check=True)
                        if t % 3 == 2:
                            mm.then_inc(scores_ready, 1)

                def transposes(i, m):
                    pe.wait_ge(probs_ready, i * 2 + m + 1)
                    for g in range(6):
                        if g >= 2:
                            pe.wait_ge(t_stored_s if g % 2 else t_stored_v, i * 6 + 3 * m + g // 2)
                        for j in range(3):
                            mm = pe.transpose(ps[0:SC, 3 * m + g % 2, bass.ts(j, 128)],
                                              probs[:, m, 3 * (g % 3) + j, bass.ts(g // 3, SC)], eye[:, :])
                        mm.then_inc(t_ready, 1)

                def context(i, m):
                    pe.wait_ge(t_stored_v, i * 6 + 3 * m + 3)
                    pe.wait_ge(t_stored_s, i * 6 + 3 * m + 3)
                    pe.wait_ge(v_stored, i + 1)
                    for j in range(4):
                        n = 0
                        for odd in range(2):
                            for c in range(2):
                                mm = pe.matmul(ps[32 * j:32 * j + 32, 3 * m + 2, 0:L],
                                               v[:, 2 * m + c, odd, bass.ts(j, 32)],
                                               probs_t[:, m, c, bass.ts(2 * j + odd, L)],
                                               start=(n == 0), stop=(n == 3))
                                n += 1
                    mm.then_inc(ctx_ready, 1)

                def project(i):
                    pe.wait_ge(ctx_stored, i * 2 + 2)
                    pe.matmul(ps[:, 2, 0:PAIR], wd_sb[:, :], ctx_sb[:, :], start=True, stop=True).then_inc(o_ready, 1)

                def step(i, last):
                    values(i)
                    scores(i, 0)
                    scores(i, 1)
                    if not last:
                        y_products(i + 1, False)
                    transposes(i, 0)
                    context(i, 0)
                    transposes(i, 1)
                    context(i, 1)
                    project(i)

                y_products(0, True)
                with pe.Fori(0, PAIRS - 1) as i:
                    step(i, False)
                step(PAIRS - 1, True)

            @block.scalar
            def _(act):
                def step(i):
                    for m in range(2):
                        for t in range(QT):
                            act.wait_ge(max_ready, i * 6 + 3 * m + t // 3 + 1)
                            a = act.activation(probs[:, m, t, :], ps[:, 3 * m + t // 3, bass.ts(t % 3, L)], ACT.Exp,
                                               bias=neg_max[:, m, t:t + 1], accum_out=row_sum[:, m, t:t + 1])
                        a.then_inc(exp_done, 1)
                    for m in range(2):
                        for g in range(1, 6, 2):
                            act.wait_ge(t_ready, i * 12 + 6 * m + g + 1)
                            act.activation(probs_t[:, m, g // 3, bass.ts(g % 3, 384)],
                                           ps[0:SC, 3 * m + 1, 0:384], ACT.Copy).then_inc(t_stored_s, 1)
                        act.wait_ge(ctx_ready, i * 2 + m + 1)
                        act.activation(ctx_sb[:, bass.ts(m, L)], ps[:, 3 * m + 2, 0:L], ACT.Copy).then_inc(ctx_stored, 1)

                with act.Fori(0, PAIRS) as i:
                    step(i)

            @block.vector
            def _(dve):
                def store_y(i):
                    for h in range(H):
                        dve.wait_ge(y_ready, i * H + h + 1)
                        dve.tensor_scalar(y[:, :, bass.ts(h, L)],
                                          ps[:, 7 - h % 2, 0:PAIR].rearrange("p (m l) -> p m l", m=2),
                                          wb4[:, h:h + 1], None, ALU.add).then_inc(y_stored, 1)

                def copy_x(i):
                    src = xn[:, bass.ds(i * PAIR, PAIR)]
                    dve.tensor_scalar(x_st[:, :], src, 1.0, None, ALU.mult)
                    dve.tensor_scalar(x_hi[:, :], src, 1.0, None, ALU.mult).then_inc(x_high, 1)

                def step(i, last):
                    dve.wait_ge(v_ready, i + 1)
                    if not last:
                        copy_x(i + 1)
                    dve.wait_ge(v_zero, 1)
                    values = ps[0:SC, 6, :].rearrange("s (q j o c) -> s q j o c", q=4, j=4, o=2)
                    kept = v[:, :, :, :].rearrange("s q p (j o c) -> s q p j o c", j=4, o=2)
                    dve.tensor_copy(kept[:, :, 0, :, 0, :], values[:, :, :, 0, :])
                    dve.tensor_copy(kept[:, :, 1, :, 1, :], values[:, :, :, 1, :]).then_inc(v_stored, 1)
                    for m in range(2):
                        for t in range(3):
                            dve.wait_ge(scores_ready, i * 6 + 3 * m + t + 1)
                            dve.tensor_reduce(neg_max[:, m, 3 * t:3 * t + 3],
                                              ps[:, 3 * m + t, 0:3 * L].rearrange("p (a l) -> p a l", a=3),
                                              AX.X, ALU.max, negate=True).then_inc(max_ready, 1)
                    dve.wait_ge(exp_done, i * 2 + 1)
                    dve.reciprocal(inv_sum[:, 0, :], row_sum[:, 0, :]).then_inc(inv_ready, 1)
                    if not last:
                        store_y(i + 1)
                    dve.wait_ge(exp_done, i * 2 + 2)
                    dve.reciprocal(inv_sum[:, 1, :], row_sum[:, 1, :]).then_inc(inv_ready, 1)
                    for m in range(2):
                        for g in range(0, 6, 2):
                            dve.wait_ge(t_ready, i * 12 + 6 * m + g + 1)
                            dve.tensor_copy(probs_t[:, m, g // 3, bass.ts(g % 3, 384)],
                                            ps[0:SC, 3 * m, 0:384]).then_inc(t_stored_v, 1)
                    dve.wait_ge(o_ready, i + 1)
                    cols_ = resid[:, bass.ds(i * PAIR, PAIR)]
                    dve.scalar_tensor_tensor(cols_, ps[:, 2, 0:PAIR], col_sb[:, 2:3], cols_,
                                             ALU.add, ALU.add).then_inc(added, 1)

                dve.memset(v[:, :, :, :], 0.0).then_inc(v_zero, 1)
                copy_x(0)
                store_y(0)
                with dve.Fori(0, PAIRS - 1) as i:
                    step(i, False)
                step(PAIRS - 1, True)

        norm_stage(nc, "norm2", resid, xn, mean_w, eps)

        with ExitStack() as ctx:
            def sb4(name, shape, dt=F32):
                return ctx.enter_context(nc.sbuf_tensor(name, shape, dt))

            def sem(name):
                return ctx.enter_context(nc.semaphore(name))

            N = 3
            Q = N * TC // 128
            W = E + 8
            log_sb = sb4("log_sb", [E, N, TC])
            aff = sb4("aff", [128, Q, E])
            score = sb4("score", [128, Q, W])
            top = sb4("top", [128, Q, 8])
            wanted = sb4("wanted", [128, Q, 8])
            left = sb4("left", [128, Q, W])
            picked = sb4("picked", [128, Q, E])
            total = sb4("total", [128, Q])
            total_eps = sb4("total_eps", [128, Q])
            inv = sb4("inv", [128, Q])
            gate = sb4("gate", [128, Q, E])
            gate_t_sb = sb4("gate_t_sb", [E, N, TC])
            log_ps = ctx.enter_context(nc.psum_tensor("log_ps", [E, N, TC], F32))
            tok_ps = ctx.enter_context(nc.psum_tensor("tok_ps", [128, 512], F32))
            gate_ps = ctx.enter_context(nc.psum_tensor("gate_ps", [E, N, TC], F32))
            log_ready = sem("log_ready")
            log_stored = sem("log_stored")
            tok_ready = sem("tok_ready")
            aff_ready = sem("aff_ready")
            dve_step = sem("dve_step")
            gate_ready = sem("gate_ready")
            gate_turned = sem("gate_turned")
            gate_stored = sem("gate_stored")
            gate_out = sem("gate_out")
            block = ctx.enter_context(nc.Block())
            STEPS = TILES // N

            @block.tensor
            def _(pe):
                with pe.Fori(0, STEPS) as i:
                    for k in range(N):
                        pe.matmul(log_ps[:, k, :], gw_sb[:, :], xn[:, bass.ds(i * (N * TC) + k * TC, TC)],
                                  start=True, stop=True).then_inc(log_ready, 1)
                    for k in range(N):
                        pe.wait_ge(log_stored, i * N + k + 1)
                        for j in range(4):
                            mm = pe.matmul(tok_ps[:, bass.ts(4 * k + j, E)], log_sb[:, k, bass.ts(j, 128)],
                                           eye[0:E, 0:E], start=True, stop=True, skip_group_check=True)
                    mm.then_inc(tok_ready, 1)
                    pe.wait_ge(gate_ready, i + 1)
                    for k in range(N):
                        for j in range(4):
                            mm = pe.transpose(gate_ps[:, k, bass.ts(j, 128)], gate[:, 4 * k + j, :], eye[:, :])
                        mm.then_inc(gate_turned, 1)

            @block.scalar
            def _(act):
                with act.Fori(0, STEPS) as i:
                    for k in range(N):
                        act.wait_ge(log_ready, i * N + k + 1)
                        act.activation(log_sb[:, k, :], log_ps[:, k, :], ACT.Copy).then_inc(log_stored, 1)
                    act.wait_ge(tok_ready, i + 1)
                    act.activation(aff[:, :, :], tok_ps[:, 0:Q * E].rearrange("p (q e) -> p q e", e=E),
                                   ACT.Sigmoid).then_inc(aff_ready, 1)
                    act.wait_ge(gate_out, i * 16)
                    for k in range(N):
                        act.wait_ge(gate_turned, i * N + k + 1)
                        act.activation(gate_t_sb[:, k, :], gate_ps[:, k, :], ACT.Copy).then_inc(gate_stored, 1)

            @block.vector
            def _(dve):
                dve.memset(score[:, :, :], LOWEST)
                dve.memset(wanted[:, :, :], LOWEST).then_inc(dve_step, 1)
                dve.wait_ge(dve_step, 1)
                CH = 8
                with dve.Fori(0, STEPS) as i:
                    base = i * CH + 1
                    dve.wait_ge(aff_ready, i + 1)
                    dve.tensor_tensor(score[:, :, 0:E], aff[:, :, :],
                                      eb_sb[:, :].unsqueeze(1).broadcast_to([128, Q, E]), ALU.add).then_inc(dve_step, 1)
                    dve.wait_ge(dve_step, base + 1)
                    dve.memset(total_eps[:, :], 0.0)
                    for q in range(Q):
                        a = dve.max(top[:, q, :], score[:, q, 0:E])
                    a.then_inc(dve_step, 1)
                    dve.wait_ge(dve_step, base + 2)
                    dve.tensor_copy(wanted[:, :, 0:TOPK], top[:, :, 0:TOPK]).then_inc(dve_step, 1)
                    dve.wait_ge(dve_step, base + 3)
                    dve.memset(inv[:, :], 0.0)
                    for q in range(Q):
                        a = dve.match_replace(left[:, q, :], wanted[:, q, :], score[:, q, :], LOWEST)
                    a.then_inc(dve_step, 1)
                    dve.wait_ge(dve_step, base + 4)
                    dve.scalar_tensor_tensor(picked[:, :, :], left[:, :, 0:E], LOWEST, aff[:, :, :],
                                             ALU.is_le, ALU.mult).then_inc(dve_step, 1)
                    dve.wait_ge(dve_step, base + 5)
                    dve.tensor_reduce(total[:, :], picked[:, :, :], AX.X, ALU.add).then_inc(dve_step, 1)
                    dve.wait_ge(dve_step, base + 6)
                    dve.tensor_scalar(total_eps[:, :], total[:, :], 1e-9, None, ALU.add).then_inc(dve_step, 1)
                    dve.wait_ge(dve_step, base + 7)
                    dve.reciprocal(inv[:, :], total_eps[:, :]).then_inc(dve_step, 1)
                    dve.wait_ge(dve_step, base + 8)
                    dve.wait_ge(gate_turned, i * N)
                    dve.tensor_tensor(gate[:, :, :], picked[:, :, :],
                                      inv[:, :].unsqueeze(2).broadcast_to([128, Q, E]), ALU.mult).then_inc(gate_ready, 1)

            @block.sync
            def _(sp):
                with sp.Fori(0, STEPS) as i:
                    sp.wait_ge(gate_stored, i * N + N)
                    sp.dma_start(gates_dram[bass.ds(i * N, N)].rearrange("k e c -> e k c"),
                                 gate_t_sb[:, :, :]).then_inc(gate_out, 16)
                sp.wait_ge(gate_out, STEPS * 16)

        with ExitStack() as ctx:
            def sb5(name, shape, dt=F32):
                return ctx.enter_context(nc.sbuf_tensor(name, shape, dt))

            def sem(name):
                return ctx.enter_context(nc.semaphore(name))

            f_hi = sb5("f_hi", [D, 2, TC], F32R)
            f_lo = sb5("f_lo", [D, 2, TC], F32R)
            gates = sb5("gates", [D, E, TC])
            silu = sb5("silu", [D, 2, TC])
            hidden = sb5("hidden", [D, 2, TC])
            result = sb5("result", [D, 2, TC])
            gate_ps = ctx.enter_context(nc.psum_tensor("g_ps", [D, 2, TC], F32))
            up_ps = ctx.enter_context(nc.psum_tensor("u_ps", [D, 2, TC], F32))
            acc_ps = ctx.enter_context(nc.psum_tensor("acc_ps", [D, 2, TC], F32))
            tile_split = sem("tile_split")
            tile_high = sem("tile_high")
            gates_in = [sem(f"gates_in{c}") for c in range(E // GC)]
            g_ready = sem("g_ready")
            u_ready = sem("u_ready")
            silu_done = sem("silu_done")
            gated = sem("gated")
            hidden_ready = sem("hidden_ready")
            down_done = sem("down_done")
            result_ready = sem("result_ready")
            result_out = [sem("result_out0"), sem("result_out1")]
            block = ctx.enter_context(nc.Block())
            STEPS = TILES // 2

            @block.sync
            def _(sp):
                def load(i, s):
                    for c in range(E // GC):
                        after(sp, gated, (i * 2 + s - 1) * E + (c + 1) * GC if s or not isinstance(i, int) else 0)
                        src = gates_dram[bass.ds(i * 2 + s, 1), bass.ts(c, GC), :].rearrange("o e t -> (o e) t")
                        sp.dma_start(gates[:, bass.ts(c, GC), :], src.partition_broadcast(D)).then_inc(gates_in[c], 16)

                load(0, 0)
                load(0, 1)
                with sp.Fori(1, STEPS) as i:
                    load(i, 0)
                    load(i, 1)

            @block.gpsimd
            def _(pool):
                def apply_gates(i, s):
                    for e in range(1, NE):
                        if (e - 1) % GC == 0:
                            pool.wait_ge(gates_in[(e - 1) // GC], i * 32 + s * 16 + 16)
                        pool.wait_ge(silu_done, i * (2 * NE) + s * NE + e + 1)
                        b = (s * NE + e) % 2
                        pool.tensor_tensor(silu[:, b, :], silu[:, b, :], gates[:, e - 1, :],
                                           ALU.mult).then_inc(gated, 1)

                with pool.Fori(0, STEPS) as i:
                    apply_gates(i, 0)
                    apply_gates(i, 1)

            @block.tensor
            def _(pe):
                def gate_up(i, s, e):
                    n = i * (2 * NE) + s * NE + e
                    b = (s * NE + e) % 2
                    for w, dst, freed, ready in ((0, gate_ps, silu_done, g_ready), (D, up_ps, hidden_ready, u_ready)):
                        after(pe, freed, n - 1)
                        out_ = dst[:, b, :]
                        pe.matmul(out_, gu_hi[:, e, w:w + D], f_hi[:, s, :], start=True, stop=False)
                        pe.matmul(out_, gu_hi[:, e, w:w + D], f_lo[:, s, :], start=False, stop=False)
                        pe.matmul(out_, gu_lo[:, e, w:w + D], f_hi[:, s, :], start=False,
                                  stop=True).then_inc(ready, 1)

                def down_product(i, s, e):
                    if e == 0:
                        after(pe, result_ready, i * 2 + s - 1)
                    pe.wait_ge(hidden_ready, i * (2 * NE) + s * NE + e + 1)
                    pe.matmul(acc_ps[:, s, :], down[:, e, :], hidden[:, (s * NE + e) % 2, :], start=(e == 0),
                              stop=(e == NE - 1)).then_inc(down_done, 1)

                def step(i):
                    for s in range(2):
                        pe.wait_ge(tile_split, i * 2 + s + 1)
                        for e in range(NE):
                            gate_up(i, s, e)
                            if e >= 1:
                                down_product(i, s, e - 1)
                            elif s == 1:
                                down_product(i, 0, NE - 1)
                            elif not isinstance(i, int) or i > 0:
                                down_product(i - 1, 1, NE - 1)

                step(0)
                with pe.Fori(1, STEPS) as i:
                    step(i)
                down_product(STEPS - 1, 1, NE - 1)

            @block.scalar
            def _(act):
                def send(i, s):
                    act.wait_ge(result_ready, i * 2 + s + 1)
                    act.dma_start(out[:, bass.ds(i * (2 * TC) + s * TC, TC)], result[:, s, :]).then_inc(result_out[s], 16)

                def step(i):
                    for s in range(2):
                        for e in range(NE):
                            n = i * (2 * NE) + s * NE + e
                            act.wait_ge(g_ready, n + 1)
                            after(act, hidden_ready, n - 1)
                            b = (s * NE + e) % 2
                            act.activation(silu[:, b, :], gate_ps[:, b, :], ACT.Silu).then_inc(silu_done, 1)
                            if e == 4:
                                if s == 1:
                                    send(i, 0)
                                elif not isinstance(i, int) or i > 0:
                                    send(i - 1, 1)

                step(0)
                with act.Fori(1, STEPS) as i:
                    step(i)
                send(STEPS - 1, 1)
                for s in range(2):
                    act.wait_ge(result_out[s], STEPS * 16)

            @block.vector
            def _(dve):
                def split(i, s):
                    src = xn[:, bass.ds(i * (2 * TC) + s * TC, TC)]
                    after(dve, u_ready, (i * 2 + s - 1) * NE)
                    dve.tensor_scalar(f_hi[:, s, :], src, 1.0, None, ALU.mult).then_inc(tile_high, 1)
                    dve.wait_ge(tile_high, i * 2 + s + 1)
                    dve.tensor_tensor(f_lo[:, s, :], src, f_hi[:, s, :].bitcast(F32),
                                      ALU.subtract).then_inc(tile_split, 1)

                def store(i, s):
                    dve.wait_ge(down_done, i * (2 * NE) + (s + 1) * NE)
                    after(dve, result_out[s], i * 16)
                    dve.tensor_tensor(result[:, s, :], resid[:, bass.ds(i * (2 * TC) + s * TC, TC)],
                                      acc_ps[:, s, :], ALU.add).then_inc(result_ready, 1)

                def step(i, last):
                    for s in range(2):
                        for e in range(NE):
                            n = i * (2 * NE) + s * NE + e
                            dve.wait_ge(u_ready, n + 1)
                            if e == 0:
                                dve.wait_ge(silu_done, n + 1)
                            else:
                                dve.wait_ge(gated, i * (2 * E) + s * E + e)
                            after(dve, down_done, n - 1)
                            b = (s * NE + e) % 2
                            dve.tensor_tensor(hidden[:, b, :], silu[:, b, :], up_ps[:, b, :],
                                              ALU.mult).then_inc(hidden_ready, 1)
                            if e == 1:
                                if s == 1:
                                    store(i, 0)
                                elif not isinstance(i, int) or i > 0:
                                    store(i - 1, 1)
                            if e == 2:
                                if s == 0:
                                    split(i, 1)
                                elif not last:
                                    split(i + 1, 0)

                split(0, 0)
                step(0, False)
                with dve.Fori(1, STEPS - 1) as i:
                    step(i, False)
                step(STEPS - 1, True)
                store(STEPS - 1, 1)


def kernel(**inputs):
    import numpy as np
    import concourse.bacc as bacc
    from concourse.bass_utils import run_bass_kernel_spmd

    a = {k: np.asarray(v) for k, v in inputs.items()}
    x = a["x"].reshape(B // IMG_LOAD, IMG_LOAD, 3, 11, 16, 13, 16)
    x = x.transpose(0, 4, 6, 2, 1, 3, 5).reshape(B // IMG_LOAD, PK, 128, IMG_LOAD * NP).transpose(0, 2, 1, 3)
    cols = np.concatenate([a["L0_tok_b"][:, None], a["L0_tok_cls_token"].reshape(D, 1), a["L0_attn_bd"][:, None],
                           a["L0_attn_mixing"].T, a["L0_attn_Wb"].T], axis=1)
    gu = np.concatenate([a["L0_ffn_shared_gate_up"][None], a["L0_ffn_expert_gate_up"]], axis=0)
    dn = np.concatenate([a["L0_ffn_shared_down"][None], a["L0_ffn_expert_down"]], axis=0)
    laid = {
        "xp": x,
        "w_tok": a["L0_tok_W"].T.reshape(PK, 128, D),
        "cols": cols,
        "pos": a["L0_tok_pos_emb"].reshape(L),
        "wq": a["L0_attn_Wq"],
        "wk": a["L0_attn_Wk"],
        "wv_t": a["L0_attn_Wv"].T,
        "wd_t": a["L0_attn_Wd"].T,
        "gate_t": a["L0_ffn_gate_w"].T,
        "ebias": a["L0_ffn_expert_bias"],
        "egu_t": gu.transpose(2, 0, 1),
        "ed_t": dn.transpose(2, 0, 1),
        "ident": np.eye(D, dtype=np.float32),
    }
    nc = bacc.Bacc("TRN2", target_bir_lowering=False, num_devices=1)
    arrays, args = {}, []
    for name, v in laid.items():
        arrays[name] = np.ascontiguousarray(v)
        args.append(nc.dram_tensor(name, arrays[name].shape, F32, kind="ExternalInput").ap())
    out = nc.dram_tensor("out", (D, T), F32, kind="ExternalOutput").ap()
    tower(nc, *args, out)
    r = run_bass_kernel_spmd(nc, [arrays], core_ids=[0])
    return r.results[0]["out"].reshape(D, B, L).transpose(1, 2, 0)
```

```python
from contextlib import ExitStack

import concourse.bass as bass
from concourse import mybir

F32 = mybir.dt.float32
F32R = mybir.dt.float32r
I32 = mybir.dt.int32
ALU = mybir.AluOpType
ACT = mybir.ActivationFunctionType
AX = mybir.AxisListType

D = 128
B = 64
NP = 143
L = NP + 1
T = B * L
PK = 6
IMG_LOAD = 4
H = 8
DH = D // H
PAIR = 2 * L
PAIRS = B // 2
HL = H * L
QT = HL // 128
SC = L // 2
TC = 512
TILES = T // TC
E = 16
NE = E + 1
TOPK = 3
EPS = 1e-5
LOWEST = -3.0e38
XN = 4
XC = 384
XT = XN * XC
XSTEPS = T // XT


def after(eng, sem, n):
    if not isinstance(n, int) or n > 0:
        eng.wait_ge(sem, n)


def norm_stage(nc, name, resid, xn, centre, mean_col, ones, eye, eps):
    N = 3
    Q = N * TC // 128
    STEPS = TILES // N
    with ExitStack() as ctx:
        cen = ctx.enter_context(nc.sbuf_tensor(f"{name}_cen", [D, N, TC], F32))
        sq = ctx.enter_context(nc.sbuf_tensor(f"{name}_sq", [D, N, TC], F32))
        std = ctx.enter_context(nc.sbuf_tensor(f"{name}_std", [128, Q], F32))
        inv = ctx.enter_context(nc.sbuf_tensor(f"{name}_inv", [128, Q], F32))
        diag = ctx.enter_context(nc.sbuf_tensor(f"{name}_diag", [128, Q, 128], F32))
        cen_ps = ctx.enter_context(nc.psum_tensor(f"{name}_cen_ps", [D, N, TC], F32))
        inv_ps = ctx.enter_context(nc.psum_tensor(f"{name}_inv_ps", [D, N, TC], F32))
        var_ps = ctx.enter_context(nc.psum_tensor(f"{name}_var_ps", [128, 512], F32))
        centred = ctx.enter_context(nc.semaphore(f"{name}_centred"))
        squared = ctx.enter_context(nc.semaphore(f"{name}_squared"))
        var_ready = ctx.enter_context(nc.semaphore(f"{name}_var_ready"))
        std_ready = ctx.enter_context(nc.semaphore(f"{name}_std_ready"))
        inv_ready = ctx.enter_context(nc.semaphore(f"{name}_inv_ready"))
        diag_ready = ctx.enter_context(nc.semaphore(f"{name}_diag_ready"))
        spread = ctx.enter_context(nc.semaphore(f"{name}_spread"))
        normed = ctx.enter_context(nc.semaphore(f"{name}_normed"))
        block = ctx.enter_context(nc.Block())

        @block.tensor
        def _(pe):
            def centring(i):
                for k in range(N):
                    after(pe, squared, (i - 1) * N + k + 1)
                    pe.matmul(cen_ps[:, k, :], centre[:, :], resid[:, bass.ds(i * (N * TC) + k * TC, TC)],
                              start=True, stop=True).then_inc(centred, 1)

            def step(i, last):
                after(pe, std_ready, i)
                for k in range(N):
                    pe.wait_ge(squared, i * N + k + 1)
                    for q in range(4 * k, 4 * k + 4):
                        mm = pe.matmul(var_ps[:, q:q + 1], sq[:, k, bass.ts(q % 4, 128)], mean_col[:, :],
                                       start=True, stop=True, skip_group_check=True)
                mm.then_inc(var_ready, 1)
                if not last:
                    centring(i + 1)
                for k in range(N):
                    pe.wait_ge(diag_ready, i * N + k + 1)
                    after(pe, normed, (i - 1) * N + k + 1)
                    for q in range(4 * k, 4 * k + 4):
                        mm = pe.matmul(inv_ps[:, k, bass.ts(q % 4, 128)], ones[:, :], diag[:, q, :],
                                       start=True, stop=True, skip_group_check=True)
                    mm.then_inc(spread, 1)

            centring(0)
            step(0, False)
            with pe.Fori(1, STEPS - 1) as i:
                step(i, False)
            step(STEPS - 1, True)

        @block.scalar
        def _(act):
            def step(i):
                for k in range(N):
                    act.wait_ge(centred, i * N + k + 1)
                    after(act, normed, (i - 1) * N + k + 1)
                    act.activation(cen[:, k, :], cen_ps[:, k, :], ACT.Copy)
                    after(act, var_ready, i)
                    act.activation(sq[:, k, :], cen_ps[:, k, :], ACT.Square).then_inc(squared, 1)
                act.wait_ge(var_ready, i + 1)
                after(act, inv_ready, i)
                act.activation(std[:, :], var_ps[:, 0:Q], ACT.Sqrt, bias=eps[:, 0:1]).then_inc(std_ready, 1)

            step(0)
            with act.Fori(1, STEPS) as i:
                step(i)

        @block.vector
        def _(dve):
            def step(i):
                dve.wait_ge(std_ready, i + 1)
                dve.reciprocal(inv[:, :], std[:, :]).then_inc(inv_ready, 1)
                dve.wait_ge(inv_ready, i + 1)
                for k in range(N):
                    after(dve, spread, (i - 1) * N + k + 1)
                    for q in range(4 * k, 4 * k + 4):
                        a = dve.tensor_scalar(diag[:, q, :], eye[:, :], inv[:, q:q + 1], None, ALU.mult)
                    a.then_inc(diag_ready, 1)
                for k in range(N):
                    dve.wait_ge(spread, i * N + k + 1)
                    dve.tensor_tensor(xn[:, bass.ds(i * (N * TC) + k * TC, TC)], cen[:, k, :],
                                      inv_ps[:, k, :], ALU.mult).then_inc(normed, 1)

            step(0)
            with dve.Fori(1, STEPS) as i:
                step(i)


def tower(nc, xp, w_tok, cols, pos, wq, wk, wv_t, wd_t, gate_t, ebias, egu_t, ed_t, ident, centring, powers, out):
    G4 = IMG_LOAD * NP
    outer = ExitStack()
    with outer:
        def sb(name, shape, dt=F32):
            return outer.enter_context(nc.sbuf_tensor(name, shape, dt))

        resid = sb("resid", [D, T])
        xn = sb("xn", [D, T])
        gu_hi = sb("gu_hi", [D, NE, 2 * D], F32R)
        gu_lo = sb("gu_lo", [D, NE, 2 * D], F32R)
        down = sb("down", [D, NE, D])
        b_hi = sb("b_hi", [D, H, D], F32R)
        b_lo = sb("b_lo", [D, H, D], F32R)
        centre = sb("centre", [D, D])
        mean_col = sb("mean_col", [D, 1])
        ones = sb("ones", [D, D])
        eps = sb("eps", [D, 1])
        eye = sb("eye", [D, D])
        wv_sb = sb("wv_sb", [D, D])
        wd_sb = sb("wd_sb", [D, D])
        gw_sb = sb("gw_sb", [D, E])
        eb_sb = sb("eb_sb", [128, E])
        col_sb = sb("col_sb", [D, 3 + 2 * H])
        wb4 = sb("wb4", [D, H])
        pow_sb = sb("pow_sb", [1, E])
        active = sb("active", [1, XSTEPS], I32)
        gates_dram = nc.dram_tensor("gates_dram", (XSTEPS, E, XT), F32, kind="Internal").ap()

        with ExitStack() as ctx:
            def sb2(name, shape, dt=F32):
                return ctx.enter_context(nc.sbuf_tensor(name, shape, dt))

            def sem(name):
                return ctx.enter_context(nc.semaphore(name))

            patches = sb2("patches", [128, 2, PK, G4])
            wt_sb = sb2("wt_sb", [128, PK, D])
            posb = sb2("posb", [D, L])
            gu_raw = sb2("gu_raw", [D, NE, 2 * D])
            wq_sb = sb2("wq_sb", [D, D])
            wk_sb = sb2("wk_sb", [D, D])
            wkm = sb2("wkm", [D, H, D])
            emb_ps = ctx.enter_context(nc.psum_tensor("emb_ps", [D, 4, 512], F32))
            b_ps = ctx.enter_context(nc.psum_tensor("b_ps", [D, 2, 512], F32))

            wt_in = sem("wt_in")
            attn_in = sem("attn_in")
            pos_in = sem("pos_in")
            gu_in = sem("gu_in")
            rest_in = sem("rest_in")
            load_in = [sem("load_in0"), sem("load_in1")]
            mm_done = sem("mm_done")
            posb_ready = sem("posb_ready")
            stored = sem("stored")
            wkm_ready = sem("wkm_ready")
            b_ready = sem("b_ready")
            b_high = sem("b_high")
            b_low = sem("b_low")
            gu_high = sem("gu_high")
            consts = sem("consts")
            block = ctx.enter_context(nc.Block())
            LOADS = B // IMG_LOAD

            @block.sync
            def _(sp):
                sp.dma_start(wt_sb[:, :, :], w_tok.rearrange("k p d -> p k d")).then_inc(wt_in, 16)
                sp.dma_start(col_sb[:, :], cols).then_inc(pos_in, 16)
                sp.dma_start(posb[:, :], pos.partition_broadcast(D)).then_inc(pos_in, 16)

                def load(i):
                    for s in range(2):
                        after(sp, mm_done, (i - 1) * 4 + 2 * s + 2)
                        sp.dma_start(patches[:, s, :, :],
                                     xp[bass.ds(i * 2 + s, 1)].rearrange("o p k n -> (o p) k n")).then_inc(load_in[s], 16)

                load(0)
                with sp.Fori(1, LOADS // 2) as i:
                    load(i)

            @block.scalar
            def _(act):
                act.dma_start(wq_sb[:, :], wq).then_inc(attn_in, 16)
                act.dma_start(wk_sb[:, :], wk).then_inc(attn_in, 16)
                act.dma_start(wv_sb[:, :], wv_t).then_inc(rest_in, 16)
                act.dma_start(wd_sb[:, :], wd_t).then_inc(rest_in, 16)
                act.dma_start(gw_sb[:, :], gate_t).then_inc(rest_in, 16)
                act.dma_start(eye[:, :], ident).then_inc(rest_in, 16)
                act.dma_start(centre[:, :], centring).then_inc(rest_in, 16)
                act.dma_start(eb_sb[:, :], ebias.partition_broadcast(128)).then_inc(rest_in, 16)
                act.dma_start(pow_sb[:, :], powers).then_inc(rest_in, 16)
                act.dma_start(gu_raw[:, :, :], egu_t).then_inc(gu_in, 16)
                act.dma_start(down[:, :, :], ed_t).then_inc(rest_in, 16)
                for h in range(0, H, 4):
                    act.wait_ge(b_ready, h // 4 + 1)
                    act.activation(b_hi[:, h:h + 4, :], b_ps[:, h // 4, :].rearrange("p (a b) -> p a b", a=4),
                                   ACT.Copy).then_inc(b_high, 1)
                act.wait_ge(gu_in, 16)
                for e in range(NE):
                    act.activation(gu_hi[:, e, :], gu_raw[:, e, :], ACT.Copy).then_inc(gu_high, 1)
                act.wait_ge(rest_in, 16 * 8)

            @block.gpsimd
            def _(pool):
                pool.memset(mean_col[:, :], 1.0 / D)
                pool.memset(ones[:, :], 1.0)
                pool.memset(eps[:, :], EPS)
                for e in range(NE):
                    pool.wait_ge(gu_high, e + 1)
                    pool.tensor_tensor(gu_lo[:, e, :], gu_raw[:, e, :], gu_hi[:, e, :].bitcast(F32),
                                       ALU.subtract).then_inc(consts, 1)
                pool.wait_ge(consts, NE)

            @block.tensor
            def _(pe):
                for h in range(H):
                    pe.wait_ge(wkm_ready, h + 1)
                    mm = pe.matmul(b_ps[:, h // 4, bass.ts(h % 4, D)], wq_sb[:, :], wkm[:, h, :],
                                   start=True, stop=True, skip_group_check=True)
                    if h % 4 == 3:
                        mm.then_inc(b_ready, 1)
                pe.wait_ge(wt_in, 16)

                def step(i):
                    for s in range(2):
                        pe.wait_ge(load_in[s], i * 16 + 16)
                        for p in range(2):
                            after(pe, stored, (i - 1) * 4 + 2 * s + p + 1)
                            for k in range(PK):
                                mm = pe.matmul(emb_ps[:, 2 * s + p, 0:2 * NP], wt_sb[:, k, :],
                                               patches[:, s, k, bass.ts(p, 2 * NP)],
                                               start=(k == 0), stop=(k == PK - 1))
                            mm.then_inc(mm_done, 1)

                step(0)
                with pe.Fori(1, LOADS // 2) as i:
                    step(i)

            @block.vector
            def _(dve):
                dve.wait_ge(attn_in, 32)
                dve.wait_ge(pos_in, 32)
                for h in range(H):
                    dve.tensor_scalar(wkm[:, h, :], wk_sb[:, :], col_sb[:, 3 + h:4 + h], 0.25,
                                      ALU.mult, ALU.mult).then_inc(wkm_ready, 1)
                dve.tensor_scalar(wb4[:, :], col_sb[:, 3 + H:3 + 2 * H], 0.25, None, ALU.mult)
                dve.tensor_scalar(posb[:, 0:1], posb[:, 0:1], col_sb[:, 1:2], None, ALU.add).then_inc(posb_ready, 1)
                dve.tensor_scalar(posb[:, 1:L], posb[:, 1:L], col_sb[:, 0:1], None, ALU.add).then_inc(posb_ready, 1)
                for h in range(0, H, 4):
                    dve.wait_ge(b_high, h // 4 + 1)
                    dve.tensor_tensor(b_lo[:, h:h + 4, :], b_ps[:, h // 4, :].rearrange("p (a b) -> p a b", a=4),
                                      b_hi[:, h:h + 4, :].bitcast(F32), ALU.subtract).then_inc(b_low, 1)
                dve.wait_ge(posb_ready, 2)
                by_image = resid[:, :].rearrange("d (b l) -> d b l", l=L)
                dve.tensor_copy(by_image[:, :, 0], posb[:, 0:1].broadcast_to([D, B]))
                with dve.Fori(0, LOADS // 2) as i:
                    for s in range(2):
                        for p in range(2):
                            dve.wait_ge(mm_done, i * 4 + 2 * s + p + 1)
                            dve.tensor_tensor(
                                by_image[:, bass.ds(i * 8 + 4 * s + 2 * p, 2), 1:L],
                                emb_ps[:, 2 * s + p, 0:2 * NP].rearrange("d (b n) -> d b n", n=NP),
                                posb[:, 1:L].unsqueeze(1).broadcast_to([D, 2, NP]), ALU.add).then_inc(stored, 1)

        norm_stage(nc, "norm1", resid, xn, centre, mean_col, ones, eye, eps)

        with ExitStack() as ctx:
            def sb3(name, shape, dt=F32):
                return ctx.enter_context(nc.sbuf_tensor(name, shape, dt))

            def sem(name):
                return ctx.enter_context(nc.semaphore(name))

            x_st = sb3("x_st", [D, PAIR])
            x_hi = sb3("x_hi", [D, PAIR], F32R)
            x_lo = sb3("x_lo", [D, PAIR], F32R)
            y = sb3("y", [D, 2, HL])
            v = sb3("v", [SC, 2, 4, 2, D])
            probs = sb3("probs", [128, 2, 2, QT, L])
            probs_t = sb3("probs_t", [SC, 2, 2, HL])
            neg_max = sb3("neg_max", [128, 2, 2, QT])
            row_sum = sb3("row_sum", [128, 2, 2, QT])
            inv_sum = sb3("inv_sum", [128, 2, 2, QT])
            ctx_sb = sb3("ctx_sb", [D, PAIR])
            ps = ctx.enter_context(nc.psum_tensor("attn_ps", [128, 8, 512], F32))

            x_high = sem("x_high")
            split_done = sem("split_done")
            v_ready = sem("v_ready")
            v_zero = sem("v_zero")
            v_stored = sem("v_stored")
            y_ready = sem("y_ready")
            y_stored_v = sem("y_stored_v")
            y_stored_s = sem("y_stored_s")
            scores_ready = sem("scores_ready")
            max_ready = sem("max_ready")
            exp_done = sem("exp_done")
            inv_ready = sem("inv_ready")
            probs_ready = sem("probs_ready")
            t_ready = [sem("t_ready0"), sem("t_ready1")]
            t_stored_v = sem("t_stored_v")
            t_stored_s = sem("t_stored_s")
            ctx_ready = sem("ctx_ready")
            ctx_stored = sem("ctx_stored")
            o_ready = sem("o_ready")
            added = sem("added")
            block = ctx.enter_context(nc.Block())

            SECOND_HALF = [("y", 0), ("y", 1), ("t", 0, 0), ("t", 0, 1), ("y", 2), ("t", 0, 2), ("t", 0, 3),
                           ("t", 0, 4), ("t", 0, 5), ("y", 3), ("t", 1, 0), ("t", 1, 1), ("y", 4), ("c", 0),
                           ("t", 1, 2), ("t", 1, 3), ("y", 5), ("t", 1, 4), ("t", 1, 5), ("y", 6), ("y", 7), ("c", 1)]
            Y_BY_VECTOR = [0, 1, 2, 5, 7]
            T_BY_VECTOR = [(0, g) for g in range(6)] + [(1, 0), (1, 2), (1, 4)]

            def y_stored_after(eng, j, h):
                mine = h in Y_BY_VECTOR
                per_pair = len(Y_BY_VECTOR) if mine else H - len(Y_BY_VECTOR)
                before = sum((g in Y_BY_VECTOR) == mine for g in range(h + 1))
                eng.wait_ge(y_stored_v if mine else y_stored_s, j * per_pair + before)

            def t_stored_after(eng, j, m, g):
                mine = (m, g) in T_BY_VECTOR
                order = [(a, b) for a in range(2) for b in range(6) if ((a, b) in T_BY_VECTOR) == mine]
                eng.wait_ge(t_stored_v if mine else t_stored_s, j * len(order) + order.index((m, g)) + 1)

            def rounds(eng, one_round):
                for j in range(3):
                    one_round(j, j % 2)
                with eng.Fori(1, PAIRS // 2 - 1) as i:
                    one_round(i * 2 + 1, 1)
                    one_round(i * 2 + 2, 0)
                one_round(PAIRS - 1, 1)
                one_round(PAIRS, 0)

            def has(j, lo, hi):
                return not isinstance(j, int) or lo <= j <= hi

            @block.gpsimd
            def _(pool):
                def one_round(j, par):
                    if has(j, 0, PAIRS - 2):
                        low_part(j + 1)
                    if has(j, 0, PAIRS - 1):
                        for m in range(2):
                            pool.wait_ge(inv_ready, j * 2 + m + 1)
                            pool.tensor_tensor(probs[:, par, m, :, :], probs[:, par, m, :, :],
                                               inv_sum[:, par, m, :].unsqueeze(2).broadcast_to([128, QT, L]),
                                               ALU.mult).then_inc(probs_ready, 1)

                def low_part(j):
                    pool.wait_ge(x_high, j + 1)
                    pool.tensor_tensor(x_lo[:, :], x_st[:, :], x_hi[:, :].bitcast(F32),
                                       ALU.subtract).then_inc(split_done, 1)

                low_part(0)
                rounds(pool, one_round)

            @block.tensor
            def _(pe):
                def y_product(j, h):
                    if h == 0:
                        pe.wait_ge(split_done, j + 1)
                        after(pe, added, j - 2)
                    if h == 1:
                        after(pe, v_stored, j)
                    if h >= 2:
                        y_stored_after(pe, j, h - 2)
                    out_ = ps[:, 7 - h % 2, 0:PAIR]
                    pe.matmul(out_, b_hi[:, h, :], x_hi[:, :], start=True, stop=False)
                    pe.matmul(out_, b_hi[:, h, :], x_lo[:, :], start=False, stop=False)
                    pe.matmul(out_, b_lo[:, h, :], x_hi[:, :], start=False, stop=True).then_inc(y_ready, 1)

                def values(j):
                    y_stored_after(pe, j, H - 1)
                    y_stored_after(pe, j, H - 2)
                    for q in range(4):
                        mm = pe.matmul(ps[0:SC, 6, bass.ts(q, D)], x_st[:, bass.ts(q, SC)], wv_sb[:, :],
                                       start=True, stop=True, skip_group_check=True)
                    mm.then_inc(v_ready, 1)

                def project(j):
                    pe.wait_ge(ctx_stored, j * 2 + 2)
                    pe.matmul(ps[:, 7, 0:PAIR], wd_sb[:, :], ctx_sb[:, :], start=True, stop=True).then_inc(o_ready, 1)

                def scores(j, m):
                    for t in range(QT):
                        mm = pe.matmul(ps[:, 3 * m + t // 3, bass.ts(t % 3, L)], y[:, m, bass.ts(t, 128)],
                                       xn[:, bass.ds(j * PAIR + m * L, L)], start=True, stop=True,
                                       skip_group_check=True)
                        if t % 3 == 2:
                            mm.then_inc(scores_ready, 1)

                def turn(j, par, m, g):
                    if g == 0:
                        pe.wait_ge(probs_ready, j * 2 + m + 1)
                        if has(j, 0, PAIRS - 2):
                            pe.wait_ge(exp_done, (j + 1) * 2 + m + 1)
                    if g >= 2:
                        t_stored_after(pe, j, m, g - 2)
                    for k in range(3):
                        mm = pe.transpose(ps[0:SC, 3 * m + g % 2, bass.ts(k, 128)],
                                          probs[:, par, m, 3 * (g % 3) + k, bass.ts(g // 3, SC)], eye[:, :])
                    mm.then_inc(t_ready[m], 1)

                def context(j, par, m):
                    t_stored_after(pe, j, m, 4)
                    t_stored_after(pe, j, m, 5)
                    for q in range(4):
                        n = 0
                        for odd in range(2):
                            for c in range(2):
                                mm = pe.matmul(ps[32 * q:32 * q + 32, 3 * m + 2, 0:L],
                                               v[:, par, 2 * m + c, odd, bass.ts(q, 32)],
                                               probs_t[:, m, c, bass.ts(2 * q + odd, L)],
                                               start=(n == 0), stop=(n == 3))
                                n += 1
                    mm.then_inc(ctx_ready, 1)

                def one_round(j, par):
                    if has(j, 0, PAIRS - 1):
                        values(j)
                    if has(j, 2, PAIRS):
                        project(j - 2)
                    if has(j, 0, PAIRS - 1):
                        scores(j, 0)
                        scores(j, 1)
                    for what, *arg in SECOND_HALF:
                        if what == "y" and has(j, 0, PAIRS - 2):
                            y_product(j + 1, arg[0])
                        if what == "t" and has(j, 1, PAIRS):
                            turn(j - 1, 1 - par, *arg)
                        if what == "c" and has(j, 1, PAIRS):
                            context(j - 1, 1 - par, arg[0])

                for h in range(H):
                    y_product(0, h)
                rounds(pe, one_round)
                project(PAIRS - 1)

            def store_y(eng, h):
                src = ps[:, 7 - h % 2, 0:PAIR].rearrange("p (m l) -> p m l", m=2)
                dst = y[:, :, bass.ts(h, L)]
                if h in Y_BY_VECTOR:
                    eng.tensor_scalar(dst, src, wb4[:, h:h + 1], None, ALU.add).then_inc(y_stored_v, 1)
                else:
                    eng.activation(dst, src, ACT.Identity, bias=wb4[:, h:h + 1]).then_inc(y_stored_s, 1)

            def store_t(eng, m, g):
                src, dst = ps[0:SC, 3 * m + g % 2, 0:384], probs_t[:, m, g // 3, bass.ts(g % 3, 384)]
                if (m, g) in T_BY_VECTOR:
                    eng.tensor_copy(dst, src).then_inc(t_stored_v, 1)
                else:
                    eng.activation(dst, src, ACT.Identity).then_inc(t_stored_s, 1)

            def store_second_half(eng, j, par, vector, between=None):
                for n, (what, *arg) in enumerate(SECOND_HALF):
                    if n == 9 and between and has(j, 0, PAIRS - 1):
                        between()
                    if what == "y" and (arg[0] in Y_BY_VECTOR) == vector and has(j, 0, PAIRS - 2):
                        eng.wait_ge(y_ready, (j + 1) * H + arg[0] + 1)
                        store_y(eng, arg[0])
                    if what == "t" and (tuple(arg) in T_BY_VECTOR) == vector and has(j, 1, PAIRS):
                        eng.wait_ge(t_ready[arg[0]], (j - 1) * 6 + arg[1] + 1)
                        store_t(eng, *arg)
                    if what == "c" and not vector and has(j, 1, PAIRS):
                        eng.wait_ge(ctx_ready, (j - 1) * 2 + arg[0] + 1)
                        eng.activation(ctx_sb[:, bass.ts(arg[0], L)], ps[:, 3 * arg[0] + 2, 0:L],
                                       ACT.Identity).then_inc(ctx_stored, 1)

            @block.scalar
            def _(act):
                def one_round(j, par):
                    if has(j, 0, PAIRS - 1):
                        for m in range(2):
                            for t in range(QT):
                                act.wait_ge(max_ready, j * 6 + 3 * m + t // 3 + 1)
                                a = act.activation(probs[:, par, m, t, :], ps[:, 3 * m + t // 3, bass.ts(t % 3, L)],
                                                   ACT.Exp, bias=neg_max[:, par, m, t:t + 1],
                                                   accum_out=row_sum[:, par, m, t:t + 1])
                            a.then_inc(exp_done, 1)
                    store_second_half(act, j, par, False)

                for h in [h for h in range(H) if h not in Y_BY_VECTOR]:
                    act.wait_ge(y_ready, h + 1)
                    store_y(act, h)
                rounds(act, one_round)

            @block.vector
            def _(dve):
                def copy_x(j):
                    src = xn[:, bass.ds(j * PAIR, PAIR)]
                    dve.tensor_scalar(x_st[:, :], src, 1.0, None, ALU.mult)
                    dve.tensor_scalar(x_hi[:, :], src, 1.0, None, ALU.mult).then_inc(x_high, 1)

                def store_v(j, par):
                    values = ps[0:SC, 6, :].rearrange("s (q j o c) -> s q j o c", q=4, j=4, o=2)
                    kept = v[:, par, :, :, :].rearrange("s q p (j o c) -> s q p j o c", j=4, o=2)
                    dve.tensor_copy(kept[:, :, 0, :, 0, :], values[:, :, :, 0, :])
                    dve.tensor_copy(kept[:, :, 1, :, 1, :], values[:, :, :, 1, :]).then_inc(v_stored, 1)

                def add_output(j):
                    dve.wait_ge(o_ready, j + 1)
                    cols_ = resid[:, bass.ds(j * PAIR, PAIR)]
                    dve.scalar_tensor_tensor(cols_, ps[:, 7, 0:PAIR], col_sb[:, 2:3], cols_,
                                             ALU.add, ALU.add).then_inc(added, 1)

                def invert(j, par, m):
                    dve.wait_ge(exp_done, j * 2 + m + 1)
                    dve.reciprocal(inv_sum[:, par, m, :], row_sum[:, par, m, :]).then_inc(inv_ready, 1)

                def one_round(j, par):
                    if has(j, 0, PAIRS - 1):
                        dve.wait_ge(v_ready, j + 1)
                        store_v(j, par)
                    if has(j, 0, PAIRS - 2):
                        copy_x(j + 1)
                    if has(j, 2, PAIRS) and not has(j, 0, PAIRS - 1):
                        add_output(j - 2)
                    if has(j, 0, PAIRS - 1):
                        for m in range(2):
                            if m == 1 and has(j, 2, PAIRS):
                                add_output(j - 2)
                            for t in range(3):
                                dve.wait_ge(scores_ready, j * 6 + 3 * m + t + 1)
                                dve.tensor_reduce(neg_max[:, par, m, 3 * t:3 * t + 3],
                                                  ps[:, 3 * m + t, 0:3 * L].rearrange("p (a l) -> p a l", a=3),
                                                  AX.X, ALU.max, negate=True).then_inc(max_ready, 1)
                        invert(j, par, 0)
                    store_second_half(dve, j, par, True, lambda: invert(j, par, 1))

                dve.memset(v[:, :, :, :, :], 0.0).then_inc(v_zero, 1)
                dve.wait_ge(v_zero, 1)
                copy_x(0)
                for h in Y_BY_VECTOR:
                    dve.wait_ge(y_ready, h + 1)
                    store_y(dve, h)
                rounds(dve, one_round)
                add_output(PAIRS - 1)

        norm_stage(nc, "norm2", resid, xn, centre, mean_col, ones, eye, eps)

        with ExitStack() as ctx:
            def sb4(name, shape, dt=F32):
                return ctx.enter_context(nc.sbuf_tensor(name, shape, dt))

            def sem(name):
                return ctx.enter_context(nc.semaphore(name))

            N = 3
            Q = N * TC // 128
            W = E + 8
            log_sb = sb4("log_sb", [E, N, TC])
            aff = sb4("aff", [128, Q, E])
            score = sb4("score", [128, Q, W])
            top = sb4("top", [128, Q, 8])
            wanted = sb4("wanted", [128, Q, 8])
            left = sb4("left", [128, Q, W])
            chosen = sb4("chosen", [128, Q, E])
            counts = sb4("counts", [1, XSTEPS * Q * E])
            taken = sb4("taken", [1, XSTEPS, E])
            bits = sb4("bits", [1, XSTEPS, E])
            bit_sum = sb4("bit_sum", [1, XSTEPS])
            picked = sb4("picked", [128, Q, E])
            total = sb4("total", [128, Q])
            total_eps = sb4("total_eps", [128, Q])
            inv = sb4("inv", [128, Q])
            gate = sb4("gate", [128, Q, E])
            gate_t_sb = sb4("gate_t_sb", [E, N, TC])
            log_ps = ctx.enter_context(nc.psum_tensor("log_ps", [E, N, TC], F32))
            tok_ps = ctx.enter_context(nc.psum_tensor("tok_ps", [128, 512], F32))
            gate_ps = ctx.enter_context(nc.psum_tensor("gate_ps", [E, N, TC], F32))
            count_ps = ctx.enter_context(nc.psum_tensor("count_ps", [128, 512], F32))
            count_ready = sem("count_ready")
            log_ready = sem("log_ready")
            log_stored = sem("log_stored")
            tok_ready = sem("tok_ready")
            aff_ready = sem("aff_ready")
            dve_step = sem("dve_step")
            gate_ready = sem("gate_ready")
            gate_turned = sem("gate_turned")
            gate_stored = sem("gate_stored")
            gate_out = sem("gate_out")
            counted = sem("counted")
            flagged = sem("flagged")
            block = ctx.enter_context(nc.Block())
            STEPS = TILES // N

            @block.tensor
            def _(pe):
                def logits(i):
                    for k in range(N):
                        after(pe, log_stored, (i - 1) * N + k + 1)
                        pe.matmul(log_ps[:, k, :], gw_sb[:, :], xn[:, bass.ds(i * (N * TC) + k * TC, TC)],
                                  start=True, stop=True).then_inc(log_ready, 1)
                    after(pe, aff_ready, i)
                    for k in range(N):
                        pe.wait_ge(log_stored, i * N + k + 1)
                        for j in range(4):
                            mm = pe.matmul(tok_ps[:, bass.ts(4 * k + j, E)], log_sb[:, k, bass.ts(j, 128)],
                                           eye[0:E, 0:E], start=True, stop=True, skip_group_check=True)
                    mm.then_inc(tok_ready, 1)

                def turn_gates(i):
                    pe.wait_ge(gate_ready, i + 1)
                    pe.matmul(count_ps[0:1, 0:Q * E], ones[:, 0:1], chosen[:, :, :].rearrange("p q e -> p (q e)"),
                              start=True, stop=True).then_inc(count_ready, 1)
                    for k in range(N):
                        after(pe, gate_stored, (i - 1) * N + k + 1)
                        for j in range(4):
                            mm = pe.transpose(gate_ps[:, k, bass.ts(j, 128)], gate[:, 4 * k + j, :], eye[:, :])
                        mm.then_inc(gate_turned, 1)

                logits(0)
                logits(1)
                turn_gates(0)
                with pe.Fori(1, STEPS - 1) as i:
                    logits(i + 1)
                    turn_gates(i)
                turn_gates(STEPS - 1)

            @block.scalar
            def _(act):
                def affinities(i):
                    for k in range(N):
                        act.wait_ge(log_ready, i * N + k + 1)
                        after(act, tok_ready, i)
                        act.activation(log_sb[:, k, :], log_ps[:, k, :], ACT.Identity).then_inc(log_stored, 1)
                    act.wait_ge(tok_ready, i + 1)
                    after(act, gate_ready, i)
                    act.activation(aff[:, :, :], tok_ps[:, 0:Q * E].rearrange("p (q e) -> p q e", e=E),
                                   ACT.Sigmoid).then_inc(aff_ready, 1)

                def store_gates(i):
                    after(act, gate_out, i * 16)
                    for k in range(N):
                        act.wait_ge(gate_turned, i * N + k + 1)
                        act.activation(gate_t_sb[:, k, :], gate_ps[:, k, :], ACT.Identity).then_inc(gate_stored, 1)

                affinities(0)
                affinities(1)
                store_gates(0)
                with act.Fori(1, STEPS - 1) as i:
                    affinities(i + 1)
                    store_gates(i)
                store_gates(STEPS - 1)

            @block.vector
            def _(dve):
                dve.memset(score[:, :, :], LOWEST)
                dve.memset(wanted[:, :, :], LOWEST).then_inc(dve_step, 1)
                dve.wait_ge(dve_step, 1)
                CH = 8

                def keep_counts(i):
                    dve.wait_ge(count_ready, i + 1)
                    dve.tensor_scalar(counts[:, bass.ds(i * (Q * E), Q * E)],
                                      count_ps[0:1, 0:Q * E], 1.0, None, ALU.mult).then_inc(counted, 1)

                def step(i):
                    base = i * CH + 1
                    dve.wait_ge(aff_ready, i + 1)
                    dve.tensor_tensor(score[:, :, 0:E], aff[:, :, :],
                                      eb_sb[:, :].unsqueeze(1).broadcast_to([128, Q, E]), ALU.add).then_inc(dve_step, 1)
                    dve.wait_ge(dve_step, base + 1)
                    dve.memset(total_eps[:, :], 0.0)
                    for q in range(Q):
                        a = dve.max(top[:, q, :], score[:, q, 0:E])
                    a.then_inc(dve_step, 1)
                    dve.wait_ge(dve_step, base + 2)
                    dve.tensor_copy(wanted[:, :, 0:TOPK], top[:, :, 0:TOPK]).then_inc(dve_step, 1)
                    dve.wait_ge(dve_step, base + 3)
                    dve.memset(inv[:, :], 0.0)
                    for q in range(Q):
                        a = dve.match_replace(left[:, q, :], wanted[:, q, :], score[:, q, :], LOWEST)
                    a.then_inc(dve_step, 1)
                    if not isinstance(i, int) or i > 0:
                        keep_counts(i - 1)
                    dve.wait_ge(dve_step, base + 4)
                    dve.tensor_scalar(chosen[:, :, :], left[:, :, 0:E], LOWEST, None, ALU.is_le)
                    dve.scalar_tensor_tensor(picked[:, :, :], left[:, :, 0:E], LOWEST, aff[:, :, :],
                                             ALU.is_le, ALU.mult).then_inc(dve_step, 1)
                    dve.wait_ge(dve_step, base + 5)
                    dve.tensor_reduce(total[:, :], picked[:, :, :], AX.X, ALU.add).then_inc(dve_step, 1)
                    dve.wait_ge(dve_step, base + 6)
                    dve.tensor_scalar(total_eps[:, :], total[:, :], 1e-9, None, ALU.add).then_inc(dve_step, 1)
                    dve.wait_ge(dve_step, base + 7)
                    dve.reciprocal(inv[:, :], total_eps[:, :]).then_inc(dve_step, 1)
                    dve.wait_ge(dve_step, base + 8)
                    after(dve, gate_turned, i * N)
                    dve.tensor_tensor(gate[:, :, :], picked[:, :, :],
                                      inv[:, :].unsqueeze(2).broadcast_to([128, Q, E]), ALU.mult).then_inc(gate_ready, 1)

                step(0)
                with dve.Fori(1, STEPS) as i:
                    step(i)
                keep_counts(STEPS - 1)
                dve.wait_ge(counted, STEPS)
                dve.tensor_reduce(taken[:, :, :], counts[:, :].rearrange("o (s q e) -> o s e q", q=Q, e=E),
                                  AX.X, ALU.add).then_inc(flagged, 1)
                dve.wait_ge(flagged, 1)
                dve.scalar_tensor_tensor(bits[:, :, :], taken[:, :, :], 0.5,
                                         pow_sb[:, :].unsqueeze(1).broadcast_to([1, XSTEPS, E]),
                                         ALU.is_gt, ALU.mult).then_inc(flagged, 1)
                dve.wait_ge(flagged, 2)
                dve.tensor_reduce(bit_sum[:, :], bits[:, :, :], AX.X, ALU.add).then_inc(flagged, 1)
                dve.wait_ge(flagged, 3)
                dve.tensor_copy(active[:, :], bit_sum[:, :])

            @block.sync
            def _(sp):
                with sp.Fori(0, STEPS) as i:
                    sp.wait_ge(gate_stored, i * N + N)
                    sp.dma_start(gates_dram[bass.ds(i, 1)].rearrange("o e (k c) -> (o e) k c", k=N),
                                 gate_t_sb[:, :, :]).then_inc(gate_out, 16)
                sp.wait_ge(gate_out, STEPS * 16)

        with ExitStack() as ctx:
            def sb5(name, shape, dt=F32):
                return ctx.enter_context(nc.sbuf_tensor(name, shape, dt))

            def sem(name):
                return ctx.enter_context(nc.semaphore(name))

            f_hi = sb5("f_hi", [D, 2 * XT], F32R)
            f_lo = sb5("f_lo", [D, 2 * XT], F32R)
            gates = sb5("gates", [D, 2 * XT])
            silu = sb5("silu", [D, 2, XC])
            hidden = sb5("hidden", [D, XN, XC])
            down_before = sb5("down_before", [D, D])
            zeros = sb5("zeros", [D, D], F32R)
            start_note = sb5("start_note", [1, 3])
            g_ps = ctx.enter_context(nc.psum_tensor("g_ps", [D, 2, 512], F32))
            u_ps = ctx.enter_context(nc.psum_tensor("u_ps", [D, 2, 512], F32))
            acc_ps = ctx.enter_context(nc.psum_tensor("acc_ps", [D, XN, 512], F32))
            zeros_ready = sem("zeros_ready")
            tile_high = sem("tile_high")
            tile_split = sem("tile_split")
            gates_in = [sem("gates_in0"), sem("gates_in1")]
            g_ready = sem("g_ready")
            u_ready = sem("u_ready")
            silu_done = sem("silu_done")
            gated = sem("gated")
            gates_free = sem("gates_free")
            hidden_ready = sem("hidden_ready")
            down_kept = sem("down_kept")
            down_done = sem("down_done")
            stored = sem("stored")
            result_out = sem("result_out")
            block = ctx.enter_context(nc.Block())

            def over_steps(eng, shared_unit, routed_unit, counters):
                def routed_units(i):
                    used = eng.value_load(active[0:1, bass.ds(i, 1)], min_val=0, max_val=2 ** E - 1)
                    for e in range(1, NE):
                        with eng.If((used & (1 << (e - 1))) != 0):
                            routed_unit(i, e)
                            for reg, _, grows in counters:
                                eng.reg_add(reg, reg, grows)

                shared_unit(0)
                for reg, grows, _ in counters:
                    if grows:
                        eng.reg_mov(reg, grows)
                routed_units(0)
                with eng.Fori(1, XSTEPS) as i:
                    shared_unit(i)
                    for reg, grows, _ in counters:
                        if grows:
                            eng.reg_add(reg, reg, grows)
                    routed_units(i)

            @block.sync
            def _(sp):
                routed = sp.alloc_register("sp_routed")
                buf = sp.alloc_register("sp_buf")
                sp.reg_mov(routed, 0)
                sp.reg_mov(buf, 0)

                def load_gates(i, e):
                    r, b = sp.snap(routed), sp.snap(buf)
                    sp.wait_ge(gates_free, r + 1)
                    for half in range(2):
                        part = bass.ts(half, XT // 2)
                        sp.wait_ge(gates_in[half], r * 16 + 16)
                        sp.dma_start(gates[:, bass.ds(b + half * (XT // 2), XT // 2)],
                                     gates_dram[bass.ds(i, 1), e - 1, part].partition_broadcast(D)
                                     ).then_inc(gates_in[half], 16)
                    sp.reg_sub(buf, XT, buf)

                over_steps(sp, lambda i: None, load_gates, [(routed, 0, 1)])

            @block.gpsimd
            def _(pool):
                pool.memset(start_note[:, 0:1], 0.0).then_inc(gates_free, 2)
                pool.memset(start_note[:, 1:2], 0.0).then_inc(gates_in[0], 16)
                pool.memset(start_note[:, 2:3], 0.0).then_inc(gates_in[1], 16)
                for i in range(XSTEPS):
                    for s in range(XN):
                        if i >= 2:
                            pool.wait_ge(stored, (i - 2) * XN + 2)
                        src = xn[:, bass.ds(i * XT + s * XC, XC)]
                        buf = bass.ds(i % 2 * XT + s * XC, XC)
                        pool.tensor_tensor(f_hi[:, buf], src, ones[:, 0:1].broadcast_to([D, XC]),
                                           ALU.mult).then_inc(tile_high, 1)
                        pool.wait_ge(tile_high, i * XN + s + 1)
                        pool.tensor_tensor(f_lo[:, buf], src, f_hi[:, buf].bitcast(F32),
                                           ALU.subtract).then_inc(tile_split, 1)

            @block.tensor
            def _(pe):
                tiles = pe.alloc_register("pe_tiles")

                def gate_up(i, n, s, e):
                    par = i % 2 if isinstance(i, int) else i & 1
                    if e == 0:
                        pe.wait_ge(tile_split, i * XN + s + 1)
                    cols_ = bass.ds(par * XT + s * XC, XC)
                    hi, lo = f_hi[:, cols_], f_lo[:, cols_]
                    for w, dst, freed, ready in ((0, g_ps, silu_done, g_ready), (D, u_ps, hidden_ready, u_ready)):
                        after(pe, freed, n - 1)
                        out_ = dst[:, s % 2, 0:XC]
                        pe.matmul(out_, gu_hi[:, e, w:w + D], hi, start=True, stop=False)
                        pe.matmul(out_, gu_hi[:, e, w:w + D], lo, start=False, stop=False)
                        pe.matmul(out_, gu_lo[:, e, w:w + D], hi, start=False, stop=True).then_inc(ready, 1)

                def down_product(n, s, weights, start):
                    pe.wait_ge(hidden_ready, n + 1)
                    pe.matmul(acc_ps[:, s, 0:XC], weights, hidden[:, s, :], start=start, stop=False,
                              skip_group_check=True).then_inc(down_done, 1)

                def unit(i, e):
                    first = isinstance(i, int) and i == 0 and e == 0
                    base = 0 if first else pe.snap(tiles)
                    gate_up(i, base, 0, e)
                    if not first:
                        finish(base, i, e, 2)
                    gate_up(i, base + 1, 1, e)
                    if not first:
                        finish(base, i, e, 3)
                    for s in range(2):
                        gate_up(i, base + 2 + s, 2 + s, e)
                        if e == 0:
                            after(pe, stored, (i - 1) * XN + s + 1)
                        down_product(base + s, s, down[:, e, :], e == 0)
                    if e == 0:
                        if first:
                            pe.wait_ge(zeros_ready, 1)
                        for s in range(2, XN):
                            after(pe, stored, (i - 1) * XN + s + 1)
                            par = i % 2 if isinstance(i, int) else i & 1
                            pe.matmul(acc_ps[:, s, 0:XC], zeros[:, :],
                                      f_hi[:, bass.ds(par * XT + s * XC, XC)],
                                      start=True, stop=False, skip_group_check=True)

                def finish(base, i, e, s):
                    if s == 2:
                        pe.wait_ge(down_kept, base)
                    down_product(base - XN + s, s, down_before[:, :], False)

                over_steps(pe, lambda i: unit(i, 0), unit, [(tiles, XN, XN)])
                base = pe.snap(tiles)
                finish(base, 0, 0, 2)
                finish(base, 0, 0, 3)

            @block.scalar
            def _(act):
                tiles = act.alloc_register("act_tiles")

                def unit(i, e):
                    first = isinstance(i, int) and i == 0 and e == 0
                    base = 0 if first else act.snap(tiles)
                    for s in range(XN):
                        if s == XN - 1:
                            if not first:
                                act.wait_ge(down_done, base)
                            act.activation(down_before[:, :], down[:, e, :], ACT.Identity).then_inc(down_kept, XN)
                        act.wait_ge(g_ready, base + s + 1)
                        after(act, hidden_ready, base + s - 1)
                        act.activation(silu[:, s % 2, :], g_ps[:, s % 2, 0:XC], ACT.Silu).then_inc(silu_done, 1)
                    if e == 0 and not first:
                        send(i - 1)

                def send(i):
                    act.wait_ge(stored, i * XN + XN)
                    cols_ = bass.ds(i * XT, XT)
                    act.dma_start(out[:, cols_], resid[:, cols_]).then_inc(result_out, 16)

                over_steps(act, lambda i: unit(i, 0), unit, [(tiles, XN, XN)])
                send(XSTEPS - 1)
                act.wait_ge(result_out, XSTEPS * 16)

            @block.vector
            def _(dve):
                tiles = dve.alloc_register("dve_tiles")
                routed = dve.alloc_register("dve_routed")
                buf = dve.alloc_register("dve_buf")

                def store(i, s, n):
                    dve.wait_ge(down_done, n + 1)
                    cols_ = bass.ds(i * XT + s * XC, XC)
                    dve.tensor_tensor(resid[:, cols_], resid[:, cols_], acc_ps[:, s, 0:XC], ALU.add).then_inc(stored, 1)

                def make_hidden(n, s):
                    dve.wait_ge(u_ready, n + 1)
                    after(dve, down_done, n - XN + 1)
                    dve.tensor_tensor(hidden[:, s, :], silu[:, s % 2, :], u_ps[:, s % 2, 0:XC],
                                      ALU.mult).then_inc(hidden_ready, 1)

                def shared_unit(i):
                    first = isinstance(i, int)
                    base = 0 if first else dve.snap(tiles)
                    for s in range(XN):
                        if not first:
                            store(i - 1, s, base - XN + s)
                        dve.wait_ge(silu_done, base + s + 1)
                        make_hidden(base + s, s)

                def routed_unit(i, e):
                    base = dve.snap(tiles)
                    r = dve.snap(routed)
                    b = dve.snap(buf)
                    for s in range(XN):
                        dve.wait_ge(silu_done, base + s + 1)
                        if s % 2 == 0:
                            dve.wait_ge(gates_in[s // 2], r * 16 + 32)
                        last = s == XN - 1
                        dve.tensor_tensor(silu[:, s % 2, :], silu[:, s % 2, :],
                                          gates[:, bass.ds(b + s * XC, XC)],
                                          ALU.mult).then_inc(gates_free if last else gated, 1)
                        if last:
                            dve.wait_ge(gates_free, r + 3)
                        else:
                            dve.wait_ge(gated, r * (XN - 1) + s + 1)
                        make_hidden(base + s, s)
                    dve.reg_sub(buf, XT, buf)

                dve.tensor_scalar(zeros[:, :], ones[:, :], 0.0, None, ALU.mult).then_inc(zeros_ready, 1)
                dve.reg_mov(routed, 0)
                dve.reg_mov(buf, 0)
                over_steps(dve, shared_unit, routed_unit, [(tiles, XN, XN), (routed, 0, 1)])
                base = dve.snap(tiles)
                for s in range(XN):
                    store(XSTEPS - 1, s, base - XN + s)


def kernel(**inputs):
    import numpy as np
    import concourse.bacc as bacc
    from concourse.bass_utils import run_bass_kernel_spmd

    a = {k: np.asarray(v) for k, v in inputs.items()}
    x = a["x"].reshape(B // IMG_LOAD, IMG_LOAD, 3, 11, 16, 13, 16)
    x = x.transpose(0, 4, 6, 2, 1, 3, 5).reshape(B // IMG_LOAD, PK, 128, IMG_LOAD * NP).transpose(0, 2, 1, 3)
    cols = np.concatenate([a["L0_tok_b"][:, None], a["L0_tok_cls_token"].reshape(D, 1), a["L0_attn_bd"][:, None],
                           a["L0_attn_mixing"].T, a["L0_attn_Wb"].T], axis=1)
    gu = np.concatenate([a["L0_ffn_shared_gate_up"][None], a["L0_ffn_expert_gate_up"]], axis=0)
    dn = np.concatenate([a["L0_ffn_shared_down"][None], a["L0_ffn_expert_down"]], axis=0)
    laid = {
        "xp": x,
        "w_tok": a["L0_tok_W"].T.reshape(PK, 128, D),
        "cols": cols,
        "pos": a["L0_tok_pos_emb"].reshape(L),
        "wq": a["L0_attn_Wq"],
        "wk": a["L0_attn_Wk"],
        "wv_t": a["L0_attn_Wv"].T,
        "wd_t": a["L0_attn_Wd"].T,
        "gate_t": a["L0_ffn_gate_w"].T,
        "ebias": a["L0_ffn_expert_bias"],
        "egu_t": gu.transpose(2, 0, 1),
        "ed_t": dn.transpose(2, 0, 1),
        "ident": np.eye(D, dtype=np.float32),
        "centring": np.eye(D, dtype=np.float32) - np.float32(1 / D),
        "powers": (2.0 ** np.arange(E, dtype=np.float32)).reshape(1, E),
    }
    nc = bacc.Bacc("TRN2", target_bir_lowering=False, num_devices=1)
    arrays, args = {}, []
    for name, v in laid.items():
        arrays[name] = np.ascontiguousarray(v)
        args.append(nc.dram_tensor(name, arrays[name].shape, F32, kind="ExternalInput").ap())
    out = nc.dram_tensor("out", (D, T), F32, kind="ExternalOutput").ap()
    tower(nc, *args, out)
    r = run_bass_kernel_spmd(nc, [arrays], core_ids=[0])
    return r.results[0]["out"].reshape(D, B, L).transpose(1, 2, 0)
```

```python
from contextlib import ExitStack

import concourse.bass as bass
from concourse import mybir

F32 = mybir.dt.float32
F32R = mybir.dt.float32r
I32 = mybir.dt.int32
ALU = mybir.AluOpType
ACT = mybir.ActivationFunctionType
AX = mybir.AxisListType

D = 128
B = 64
NP = 143
L = NP + 1
T = B * L
PK = 6
IMG_LOAD = 2
H = 8
PAIR = 2 * L
PAIRS = B // 2
HL = H * L
QT = HL // 128
SC = L // 2
TC = 512
TILES = T // TC
E = 16
NE = E + 1
TOPK = 3
EPS = 1e-5
LOWEST = -3.0e38
XN = 4
XC = 384
XT = XN * XC
XSTEPS = T // XT


def after(eng, sem, n):
    if not isinstance(n, int) or n > 0:
        eng.wait_ge(sem, n)


def norm_stage(nc, name, resid, xn, centre, mean_col, select, eye, eps, loads=()):
    N = 3
    Q = N * TC // 128
    STEPS = TILES // N
    with ExitStack() as ctx:
        def sb(what, shape, dt=F32):
            return ctx.enter_context(nc.sbuf_tensor(f"{name}_{what}", shape, dt))

        def sem(what):
            return ctx.enter_context(nc.semaphore(f"{name}_{what}"))

        x_hi, x_lo = sb("x_hi", [D, N, TC], F32R), sb("x_lo", [D, N, TC], F32R)
        cen = sb("cen", [D, 2, N, TC])
        sq = sb("sq", [D, N, TC])
        std = sb("std", [128, Q])
        inv = sb("inv", [128, 128])
        inv_rows = sb("inv_rows", [128, 128])
        cen_ps = ctx.enter_context(nc.psum_tensor(f"{name}_cen_ps", [D, N, TC], F32))
        inv_ps = ctx.enter_context(nc.psum_tensor(f"{name}_inv_ps", [D, N, TC], F32))
        var_ps = ctx.enter_context(nc.psum_tensor(f"{name}_var_ps", [128, 512], F32))
        turn_ps = ctx.enter_context(nc.psum_tensor(f"{name}_turn_ps", [128, 512], F32))
        x_high, x_split, centred, squared = sem("x_high"), sem("x_split"), sem("centred"), sem("squared")
        var_ready, std_ready, inv_ready = sem("var_ready"), sem("std_ready"), sem("inv_ready")
        loaded = sem("loaded")
        turned, rows_ready, spread, normed = sem("turned"), sem("rows_ready"), sem("spread"), sem("normed")
        block = ctx.enter_context(nc.Block())

        def steps(eng, step):
            for i in range(2):
                step(i, i, False)
            with eng.Fori(1, STEPS // 2 - 1) as i:
                step(i * 2, 0, False)
                step(i * 2 + 1, 1, False)
            for i in range(STEPS - 2, STEPS):
                step(i, i % 2, i == STEPS - 1)

        @block.tensor
        def _(pe):
            def centring(i, k):
                pe.wait_ge(x_split, i * N + k + 1)
                after(pe, squared, (i - 1) * N + k + 1)
                pe.matmul(cen_ps[:, k, :], centre[:, :], x_hi[:, k, :], start=True, stop=False)
                pe.matmul(cen_ps[:, k, :], centre[:, :], x_lo[:, k, :], start=False, stop=True).then_inc(centred, 1)

            def step(i, par, last):
                after(pe, std_ready, i)
                for k in range(N):
                    pe.wait_ge(squared, i * N + k + 1)
                    for q in range(4 * k, 4 * k + 4):
                        mm = pe.matmul(var_ps[:, q:q + 1], sq[:, k, bass.ts(q % 4, 128)], mean_col[:, :],
                                       start=True, stop=True, skip_group_check=True)
                mm.then_inc(var_ready, 1)
                if not last:
                    centring(i + 1, 0)
                    centring(i + 1, 1)
                pe.wait_ge(inv_ready, i + 1)
                pe.transpose(turn_ps[:, 0:128], inv[:, :], eye[:, :]).then_inc(turned, 1)
                if not last:
                    centring(i + 1, 2)
                pe.wait_ge(rows_ready, i + 1)
                for k in range(N):
                    after(pe, normed, (i - 1) * N + k + 1)
                    for q in range(4 * k, 4 * k + 4):
                        mm = pe.matmul(inv_ps[:, k, bass.ts(q % 4, 128)], select[:, q, :], inv_rows[:, :],
                                       start=True, stop=True, skip_group_check=True)
                    mm.then_inc(spread, 1)

            for k in range(N):
                centring(0, k)
            steps(pe, step)

        @block.scalar
        def _(act):
            def step(i, par, last):
                for k in range(N):
                    act.wait_ge(centred, i * N + k + 1)
                    after(act, var_ready, i)
                    act.activation(sq[:, k, :], cen_ps[:, k, :], ACT.Square)
                    after(act, normed, (i - 2) * N + k + 1)
                    act.activation(cen[:, par, k, :], cen_ps[:, k, :], ACT.Copy).then_inc(squared, 1)
                act.wait_ge(var_ready, i + 1)
                after(act, inv_ready, i)
                act.activation(std[:, :], var_ps[:, 0:Q], ACT.Sqrt, bias=eps[:, 0:1]).then_inc(std_ready, 1)

            steps(act, step)

        @block.sync
        def _(sp):
            for dst, src in loads:
                sp.dma_start(dst, src).then_inc(loaded, 16)
            if loads:
                sp.wait_ge(loaded, 16 * len(loads))

        @block.gpsimd
        def _(pool):
            def low_parts(i):
                for k in range(N):
                    pool.wait_ge(x_high, i * N + k + 1)
                    pool.tensor_tensor(x_lo[:, k, :], resid[:, bass.ds(i * (N * TC) + k * TC, TC)],
                                       x_hi[:, k, :].bitcast(F32), ALU.subtract).then_inc(x_split, 1)

            low_parts(0)
            with pool.Fori(1, STEPS) as i:
                low_parts(i)

        @block.vector
        def _(dve):
            def high_parts(i):
                for k in range(N):
                    after(dve, centred, (i - 1) * N + k + 1)
                    dve.tensor_scalar(x_hi[:, k, :], resid[:, bass.ds(i * (N * TC) + k * TC, TC)], 1.0, None,
                                      ALU.mult).then_inc(x_high, 1)

            def step(i, par, last):
                dve.wait_ge(std_ready, i + 1)
                after(dve, turned, i)
                dve.reciprocal(inv[:, 0:Q], std[:, :]).then_inc(inv_ready, 1)
                dve.wait_ge(turned, i + 1)
                after(dve, spread, i * N)
                dve.tensor_copy(inv_rows[:, :], turn_ps[:, 0:128]).then_inc(rows_ready, 1)
                if not isinstance(i, int) or i < STEPS - 2:
                    high_parts(i + 2)
                for k in range(N):
                    dve.wait_ge(spread, i * N + k + 1)
                    dve.tensor_tensor(xn[:, bass.ds(i * (N * TC) + k * TC, TC)], cen[:, par, k, :],
                                      inv_ps[:, k, :], ALU.mult).then_inc(normed, 1)

            dve.memset(inv[:, Q:128], 0.0)
            high_parts(0)
            high_parts(1)
            steps(dve, step)


def tower(nc, xp, w_tok, cols, pos, wq, wk, wv_t, wd_t, gate_t, ebias, egu_t, ed_t, ident, centring, powers, out):
    LC = IMG_LOAD * NP
    outer = ExitStack()
    with outer:
        def sb(name, shape, dt=F32):
            return outer.enter_context(nc.sbuf_tensor(name, shape, dt))

        resid = sb("resid", [D, T])
        xn = sb("xn", [D, T])
        gu_hi = sb("gu_hi", [D, NE, 2 * D], F32R)
        gu_lo = sb("gu_lo", [D, NE, 2 * D], F32R)
        b_hi = sb("b_hi", [D, H, D], F32R)
        b_lo = sb("b_lo", [D, H, D], F32R)
        centre = sb("centre", [D, D], F32R)
        select = sb("select", [D, 12, D])
        mean_col = sb("mean_col", [D, 1])
        ones = sb("ones", [D, D])
        eps = sb("eps", [D, 1])
        eye = sb("eye", [D, D])
        wv_sb = sb("wv_sb", [D, D])
        wd_sb = sb("wd_sb", [D, D])
        gw_sb = sb("gw_sb", [D, E])
        eb_sb = sb("eb_sb", [128, E])
        col_sb = sb("col_sb", [D, 3 + 2 * H])
        wb4 = sb("wb4", [D, H])
        pow_sb = sb("pow_sb", [1, E])
        active = sb("active", [1, XSTEPS], I32)
        gates_dram = nc.dram_tensor("gates_dram", (XSTEPS, E, XT), F32, kind="Internal").ap()

        with ExitStack() as ctx:
            def sb2(name, shape, dt=F32):
                return ctx.enter_context(nc.sbuf_tensor(name, shape, dt))

            def sem(name):
                return ctx.enter_context(nc.semaphore(name))

            patches = sb2("patches", [128, 4, PK, LC])
            wt_sb = sb2("wt_sb", [128, PK, D])
            posb = sb2("posb", [D, L])
            centre_raw = sb2("centre_raw", [D, D])
            wq_sb = sb2("wq_sb", [D, D])
            wk_sb = sb2("wk_sb", [D, D])
            wkm = sb2("wkm", [D, H, D])
            emb_ps = ctx.enter_context(nc.psum_tensor("emb_ps", [D, 4, 512], F32))
            b_ps = ctx.enter_context(nc.psum_tensor("b_ps", [D, 2, 512], F32))

            wt_in = sem("wt_in")
            attn_in = sem("attn_in")
            pos_in = sem("pos_in")
            rest_in = sem("rest_in")
            load_in = [sem(f"load_in{s}") for s in range(4)]
            mm_done = sem("mm_done")
            posb_ready = sem("posb_ready")
            stored = sem("stored")
            wkm_ready = sem("wkm_ready")
            b_ready = sem("b_ready")
            b_high = sem("b_high")
            b_low = sem("b_low")
            block = ctx.enter_context(nc.Block())
            LOADS = B // IMG_LOAD

            @block.sync
            def _(sp):
                sp.dma_start(wt_sb[:, :, :], w_tok.rearrange("k p d -> p k d")).then_inc(wt_in, 16)
                sp.dma_start(col_sb[:, :], cols).then_inc(pos_in, 16)
                sp.dma_start(posb[:, :], pos.partition_broadcast(D)).then_inc(pos_in, 16)

                def load(i):
                    for s in range(4):
                        after(sp, mm_done, (i - 1) * 4 + s + 1)
                        sp.dma_start(patches[:, s, :, :],
                                     xp[bass.ds(i * 4 + s, 1)].rearrange("o p k n -> (o p) k n")).then_inc(load_in[s], 16)

                load(0)
                with sp.Fori(1, LOADS // 4) as i:
                    load(i)

            @block.scalar
            def _(act):
                act.dma_start(wq_sb[:, :], wq).then_inc(attn_in, 16)
                act.dma_start(wk_sb[:, :], wk).then_inc(attn_in, 16)
                act.dma_start(wv_sb[:, :], wv_t).then_inc(rest_in, 16)
                act.dma_start(wd_sb[:, :], wd_t).then_inc(rest_in, 16)
                act.dma_start(gw_sb[:, :], gate_t).then_inc(rest_in, 16)
                act.dma_start(eye[:, :], ident).then_inc(rest_in, 16)
                act.dma_start(centre_raw[:, :], centring).then_inc(rest_in, 16)
                act.dma_start(eb_sb[:, :], ebias.partition_broadcast(128)).then_inc(rest_in, 16)
                act.dma_start(pow_sb[:, :], powers).then_inc(rest_in, 16)
                for h in range(0, H, 4):
                    act.wait_ge(b_ready, h // 4 + 1)
                    act.activation(b_hi[:, h:h + 4, :], b_ps[:, h // 4, :].rearrange("p (a b) -> p a b", a=4),
                                   ACT.Copy).then_inc(b_high, 1)
                act.wait_ge(rest_in, 16 * 7)
                act.activation(centre[:, :], centre_raw[:, :], ACT.Copy)
                for q in range(12):
                    act.activation(select[:, q, :], eye[:, q:q + 1].broadcast_to([D, D]), ACT.Copy)

            @block.gpsimd
            def _(pool):
                pool.memset(mean_col[:, :], 1.0 / D)
                pool.memset(ones[:, :], 1.0)
                pool.memset(eps[:, :], EPS)

            @block.tensor
            def _(pe):
                for h in range(H):
                    pe.wait_ge(wkm_ready, h + 1)
                    mm = pe.matmul(b_ps[:, h // 4, bass.ts(h % 4, D)], wq_sb[:, :], wkm[:, h, :],
                                   start=True, stop=True, skip_group_check=True)
                    if h % 4 == 3:
                        mm.then_inc(b_ready, 1)
                pe.wait_ge(wt_in, 16)

                def step(i):
                    for s in range(4):
                        pe.wait_ge(load_in[s], i * 16 + 16)
                        after(pe, stored, (i - 1) * 4 + s + 1)
                        for k in range(PK):
                            mm = pe.matmul(emb_ps[:, s, 0:LC], wt_sb[:, k, :], patches[:, s, k, :],
                                           start=(k == 0), stop=(k == PK - 1))
                        mm.then_inc(mm_done, 1)

                step(0)
                with pe.Fori(1, LOADS // 4) as i:
                    step(i)

            @block.vector
            def _(dve):
                dve.wait_ge(attn_in, 32)
                dve.wait_ge(pos_in, 32)
                for h in range(H):
                    dve.tensor_scalar(wkm[:, h, :], wk_sb[:, :], col_sb[:, 3 + h:4 + h], 0.25,
                                      ALU.mult, ALU.mult).then_inc(wkm_ready, 1)
                dve.tensor_scalar(wb4[:, :], col_sb[:, 3 + H:3 + 2 * H], 0.25, None, ALU.mult)
                dve.tensor_scalar(posb[:, 0:1], posb[:, 0:1], col_sb[:, 1:2], None, ALU.add).then_inc(posb_ready, 1)
                dve.tensor_scalar(posb[:, 1:L], posb[:, 1:L], col_sb[:, 0:1], None, ALU.add).then_inc(posb_ready, 1)
                for h in range(0, H, 4):
                    dve.wait_ge(b_high, h // 4 + 1)
                    dve.tensor_tensor(b_lo[:, h:h + 4, :], b_ps[:, h // 4, :].rearrange("p (a b) -> p a b", a=4),
                                      b_hi[:, h:h + 4, :].bitcast(F32), ALU.subtract).then_inc(b_low, 1)
                dve.wait_ge(posb_ready, 2)
                by_image = resid[:, :].rearrange("d (b l) -> d b l", l=L)
                dve.tensor_copy(by_image[:, :, 0], posb[:, 0:1].broadcast_to([D, B]))
                with dve.Fori(0, LOADS // 4) as i:
                    for s in range(4):
                        dve.wait_ge(mm_done, i * 4 + s + 1)
                        dve.tensor_tensor(by_image[:, bass.ds(i * 8 + 2 * s, 2), 1:L],
                                          emb_ps[:, s, 0:LC].rearrange("d (b n) -> d b n", n=NP),
                                          posb[:, 1:L].unsqueeze(1).broadcast_to([D, 2, NP]), ALU.add).then_inc(stored, 1)

        norm_stage(nc, "norm1", resid, xn, centre, mean_col, select, eye, eps)

        with ExitStack() as ctx:
            def sb3(name, shape, dt=F32):
                return ctx.enter_context(nc.sbuf_tensor(name, shape, dt))

            def sem(name):
                return ctx.enter_context(nc.semaphore(name))

            x_st = sb3("x_st", [D, PAIR])
            x_hi = sb3("x_hi", [D, PAIR], F32R)
            x_lo = sb3("x_lo", [D, PAIR], F32R)
            y = sb3("y", [D, 2, 2, HL])
            v = sb3("v", [SC, 2, 4, 2, D])
            probs = sb3("probs", [128, 2, 2, QT, L])
            probs_t = sb3("probs_t", [SC, 2, 2, HL])
            neg_max = sb3("neg_max", [128, 2, 2, QT])
            row_sum = sb3("row_sum", [128, 2, 2, QT])
            inv_sum = sb3("inv_sum", [128, 2, 2, QT])
            ctx_sb = sb3("ctx_sb", [D, PAIR])
            ps = ctx.enter_context(nc.psum_tensor("attn_ps", [128, 8, 512], F32))

            x_high = sem("x_high")
            split_done = sem("split_done")
            v_ready = sem("v_ready")
            v_zero = sem("v_zero")
            v_stored = sem("v_stored")
            y_ready = sem("y_ready")
            y_stored_v = sem("y_stored_v")
            y_stored_s = sem("y_stored_s")
            scores_ready = sem("scores_ready")
            max_ready = sem("max_ready")
            exp_done = sem("exp_done")
            inv_ready = sem("inv_ready")
            probs_ready = sem("probs_ready")
            t_ready = [sem("t_ready0"), sem("t_ready1")]
            t_stored_v = sem("t_stored_v")
            t_stored_s = sem("t_stored_s")
            ctx_ready = sem("ctx_ready")
            ctx_stored = sem("ctx_stored")
            o_ready = sem("o_ready")
            added = sem("added")
            block = ctx.enter_context(nc.Block())

            ORDER = [("s", 0, 0), ("s", 0, 1), ("s", 0, 2), ("y", 0), ("s", 1, 0), ("y", 1), ("y", 2), ("s", 1, 1),
                     ("s", 1, 2), ("t", 0, 0), ("t", 0, 1), ("y", 3), ("y", 4), ("t", 0, 2), ("t", 0, 3), ("y", 5),
                     ("t", 0, 4), ("t", 0, 5), ("t", 1, 0), ("t", 1, 1), ("y", 6), ("t", 1, 2),
                     ("t", 1, 3), ("y", 7), ("t", 1, 4), ("t", 1, 5), ("c", 0), ("c", 1)]
            Y_BY_VECTOR = [0, 1, 2, 3, 4, 6]
            ADD_AT = (0, 1)
            INVERT_AFTER = [("t", 0, 3), ("t", 0, 5)]
            T_BY_VECTOR = [(0, 0), (0, 1), (0, 3), (0, 5), (1, 1), (1, 3), (1, 5)]

            def y_stored_after(eng, j, h):
                mine = h in Y_BY_VECTOR
                per_pair = len(Y_BY_VECTOR) if mine else H - len(Y_BY_VECTOR)
                before = sum((g in Y_BY_VECTOR) == mine for g in range(h + 1))
                eng.wait_ge(y_stored_v if mine else y_stored_s, j * per_pair + before)

            def t_stored_after(eng, j, m, g):
                mine = (m, g) in T_BY_VECTOR
                order = [(a, b) for a in range(2) for b in range(6) if ((a, b) in T_BY_VECTOR) == mine]
                eng.wait_ge(t_stored_v if mine else t_stored_s, j * len(order) + order.index((m, g)) + 1)

            def rounds(eng, one_round):
                for j in range(3):
                    one_round(j, j % 2)
                with eng.Fori(1, PAIRS // 2 - 1) as i:
                    one_round(i * 2 + 1, 1)
                    one_round(i * 2 + 2, 0)
                one_round(PAIRS - 1, 1)
                one_round(PAIRS, 0)

            def has(j, lo, hi):
                return not isinstance(j, int) or lo <= j <= hi

            @block.gpsimd
            def _(pool):
                def one_round(j, par):
                    if has(j, 0, PAIRS - 2):
                        low_part(j + 1)
                    if has(j, 0, PAIRS - 1):
                        for m in range(2):
                            pool.wait_ge(inv_ready, j * 2 + m + 1)
                            pool.tensor_tensor(probs[:, par, m, :, :], probs[:, par, m, :, :],
                                               inv_sum[:, par, m, :].unsqueeze(2).broadcast_to([128, QT, L]),
                                               ALU.mult).then_inc(probs_ready, 1)

                def low_part(j):
                    pool.wait_ge(x_high, j + 1)
                    pool.tensor_tensor(x_lo[:, :], x_st[:, :], x_hi[:, :].bitcast(F32),
                                       ALU.subtract).then_inc(split_done, 1)

                low_part(0)
                rounds(pool, one_round)

            @block.tensor
            def _(pe):
                def y_product(j, h):
                    if h == 0:
                        pe.wait_ge(split_done, j + 1)
                        after(pe, added, j - 2)
                    if h == 1:
                        after(pe, v_stored, j)
                    if h >= 2:
                        y_stored_after(pe, j, h - 2)
                    out_ = ps[:, 7 - h % 2, 0:PAIR]
                    pe.matmul(out_, b_hi[:, h, :], x_hi[:, :], start=True, stop=False)
                    pe.matmul(out_, b_hi[:, h, :], x_lo[:, :], start=False, stop=False)
                    pe.matmul(out_, b_lo[:, h, :], x_hi[:, :], start=False, stop=True).then_inc(y_ready, 1)

                def values(j):
                    y_stored_after(pe, j, H - 1)
                    y_stored_after(pe, j, H - 2)
                    for q in range(4):
                        mm = pe.matmul(ps[0:SC, 6, bass.ts(q, D)], x_st[:, bass.ts(q, SC)], wv_sb[:, :],
                                       start=True, stop=True, skip_group_check=True)
                    mm.then_inc(v_ready, 1)

                def project(j):
                    pe.wait_ge(ctx_stored, j * 2 + 2)
                    pe.matmul(ps[:, 7, 0:PAIR], wd_sb[:, :], ctx_sb[:, :], start=True, stop=True).then_inc(o_ready, 1)

                def scores(j, par, m, g):
                    for t in range(3 * g, 3 * g + 3):
                        mm = pe.matmul(ps[:, 3 * m + g, bass.ts(t % 3, L)], y[:, par, m, bass.ts(t, 128)],
                                       xn[:, bass.ds(j * PAIR + m * L, L)], start=True, stop=True,
                                       skip_group_check=True)
                    mm.then_inc(scores_ready, 1)

                def turn(j, par, m, g):
                    if g == 0:
                        pe.wait_ge(probs_ready, j * 2 + m + 1)
                        if has(j, 0, PAIRS - 2):
                            pe.wait_ge(exp_done, (j + 1) * 2 + m + 1)
                    if g >= 2:
                        t_stored_after(pe, j, m, g - 2)
                    for k in range(3):
                        mm = pe.transpose(ps[0:SC, 3 * m + g % 2, bass.ts(k, 128)],
                                          probs[:, par, m, 3 * (g % 3) + k, bass.ts(g // 3, SC)], eye[:, :])
                    mm.then_inc(t_ready[m], 1)

                def context(j, par, m):
                    t_stored_after(pe, j, m, 4)
                    t_stored_after(pe, j, m, 5)
                    for q in range(4):
                        n = 0
                        for odd in range(2):
                            for c in range(2):
                                mm = pe.matmul(ps[32 * q:32 * q + 32, 3 * m + 2, 0:L],
                                               v[:, par, 2 * m + c, odd, bass.ts(q, 32)],
                                               probs_t[:, m, c, bass.ts(2 * q + odd, L)],
                                               start=(n == 0), stop=(n == 3))
                                n += 1
                    mm.then_inc(ctx_ready, 1)

                def one_round(j, par):
                    if has(j, 0, PAIRS - 1):
                        values(j)
                    if has(j, 2, PAIRS):
                        project(j - 2)
                    for what, *arg in ORDER:
                        if what == "s" and has(j, 0, PAIRS - 1):
                            scores(j, par, *arg)
                        if what == "y" and has(j, 0, PAIRS - 2):
                            y_product(j + 1, arg[0])
                        if what == "t" and has(j, 1, PAIRS):
                            turn(j - 1, 1 - par, *arg)
                        if what == "c" and has(j, 1, PAIRS):
                            context(j - 1, 1 - par, arg[0])

                for h in range(H):
                    y_product(0, h)
                rounds(pe, one_round)
                project(PAIRS - 1)

            def store_y(eng, par, h):
                src = ps[:, 7 - h % 2, 0:PAIR].rearrange("p (m l) -> p m l", m=2)
                dst = y[:, par, :, bass.ts(h, L)]
                if h in Y_BY_VECTOR:
                    eng.tensor_scalar(dst, src, wb4[:, h:h + 1], None, ALU.add).then_inc(y_stored_v, 1)
                else:
                    eng.activation(dst, src, ACT.Identity, bias=wb4[:, h:h + 1]).then_inc(y_stored_s, 1)

            def store_t(eng, m, g):
                src, dst = ps[0:SC, 3 * m + g % 2, 0:384], probs_t[:, m, g // 3, bass.ts(g % 3, 384)]
                if (m, g) in T_BY_VECTOR:
                    eng.tensor_copy(dst, src).then_inc(t_stored_v, 1)
                else:
                    eng.activation(dst, src, ACT.Identity).then_inc(t_stored_s, 1)

            def store(eng, j, par, vector, what, *arg):
                if what == "y" and (arg[0] in Y_BY_VECTOR) == vector and has(j, 0, PAIRS - 2):
                    eng.wait_ge(y_ready, (j + 1) * H + arg[0] + 1)
                    store_y(eng, 1 - par, arg[0])
                if what == "t" and (tuple(arg) in T_BY_VECTOR) == vector and has(j, 1, PAIRS):
                    eng.wait_ge(t_ready[arg[0]], (j - 1) * 6 + arg[1] + 1)
                    store_t(eng, *arg)
                if what == "c" and not vector and has(j, 1, PAIRS):
                    eng.wait_ge(ctx_ready, (j - 1) * 2 + arg[0] + 1)
                    eng.activation(ctx_sb[:, bass.ts(arg[0], L)], ps[:, 3 * arg[0] + 2, 0:L],
                                   ACT.Identity).then_inc(ctx_stored, 1)

            def values_of(par, odd):
                kept = v[:, par, :, :, :].rearrange("s q p (j o c) -> s q p j o c", j=4, o=2)
                values = ps[0:SC, 6, :].rearrange("s (q j o c) -> s q j o c", q=4, j=4, o=2)
                return kept[:, :, odd, :, odd, :], values[:, :, :, odd, :]

            @block.scalar
            def _(act):
                def exponentials(j, par, m, g):
                    act.wait_ge(max_ready, j * 6 + 3 * m + g + 1)
                    for t in range(3 * g, 3 * g + 3):
                        a = act.activation(probs[:, par, m, t, :], ps[:, 3 * m + g, bass.ts(t % 3, L)],
                                           ACT.Exp, bias=neg_max[:, par, m, t:t + 1],
                                           accum_out=row_sum[:, par, m, t:t + 1])
                    if g == 2:
                        a.then_inc(exp_done, 1)

                def one_round(j, par):
                    if has(j, 0, PAIRS - 1):
                        act.wait_ge(v_ready, j + 1)
                        act.activation(*values_of(par, 0), ACT.Identity)
                        act.activation(*values_of(par, 1), ACT.Identity).then_inc(v_stored, 1)
                    for what, *arg in ORDER:
                        if what == "s" and has(j, 0, PAIRS - 1):
                            exponentials(j, par, *arg)
                        store(act, j, par, False, what, *arg)

                act.wait_ge(v_zero, 1)
                for h in [h for h in range(H) if h not in Y_BY_VECTOR]:
                    act.wait_ge(y_ready, h + 1)
                    store_y(act, 0, h)
                rounds(act, one_round)

            @block.vector
            def _(dve):
                def copy_x(j):
                    src = xn[:, bass.ds(j * PAIR, PAIR)]
                    dve.tensor_scalar(x_st[:, :], src, 1.0, None, ALU.mult)
                    dve.tensor_scalar(x_hi[:, :], src, 1.0, None, ALU.mult).then_inc(x_high, 1)

                def add_output(j):
                    dve.wait_ge(o_ready, j + 1)
                    cols_ = resid[:, bass.ds(j * PAIR, PAIR)]
                    dve.scalar_tensor_tensor(cols_, ps[:, 7, 0:PAIR], col_sb[:, 2:3], cols_,
                                             ALU.add, ALU.add).then_inc(added, 1)

                def invert(j, par, m):
                    dve.wait_ge(exp_done, j * 2 + m + 1)
                    dve.reciprocal(inv_sum[:, par, m, :], row_sum[:, par, m, :]).then_inc(inv_ready, 1)

                def one_round(j, par):
                    if has(j, 0, PAIRS - 1):
                        dve.wait_ge(v_ready, j + 1)
                    if has(j, 0, PAIRS - 2):
                        copy_x(j + 1)
                    if has(j, 2, PAIRS) and not has(j, 0, PAIRS - 1):
                        add_output(j - 2)
                    for what, *arg in ORDER:
                        if what == "s" and has(j, 0, PAIRS - 1):
                            m, g = arg
                            if (m, g) == ADD_AT and has(j, 2, PAIRS):
                                add_output(j - 2)
                            dve.wait_ge(scores_ready, j * 6 + 3 * m + g + 1)
                            dve.tensor_reduce(neg_max[:, par, m, 3 * g:3 * g + 3],
                                              ps[:, 3 * m + g, 0:3 * L].rearrange("p (a l) -> p a l", a=3),
                                              AX.X, ALU.max, negate=True).then_inc(max_ready, 1)
                        store(dve, j, par, True, what, *arg)
                        if (what, *arg) in INVERT_AFTER and has(j, 0, PAIRS - 1):
                            invert(j, par, INVERT_AFTER.index((what, *arg)))

                dve.memset(v[:, :, :, :, :], 0.0).then_inc(v_zero, 1)
                dve.wait_ge(v_zero, 1)
                copy_x(0)
                for h in Y_BY_VECTOR:
                    dve.wait_ge(y_ready, h + 1)
                    store_y(dve, 0, h)
                rounds(dve, one_round)
                add_output(PAIRS - 1)

        down_hi = sb("down_hi", [D, NE, D], F32R)
        down_lo = sb("down_lo", [D, NE, D], F32R)
        raw = ExitStack()
        gu_raw = raw.enter_context(nc.sbuf_tensor("gu_raw", [D, NE, 2 * D], F32))
        down_raw = raw.enter_context(nc.sbuf_tensor("down_raw", [D, NE, D], F32))
        norm_stage(nc, "norm2", resid, xn, centre, mean_col, select, eye, eps,
                   [(gu_raw[:, :, :], egu_t), (down_raw[:, :, :], ed_t)])

        with ExitStack() as ctx:
            def sb4(name, shape, dt=F32):
                return ctx.enter_context(nc.sbuf_tensor(name, shape, dt))

            def sem(name):
                return ctx.enter_context(nc.semaphore(name))

            N = 3
            Q = N * TC // 128
            W = E + 8
            note = sb4("note", [D, 1])
            x_copy = sb4("x_copy", [D, N, TC])
            aff = sb4("aff", [128, Q, E])
            score = sb4("score", [128, Q, W])
            top = sb4("top", [128, Q, 8])
            wanted = sb4("wanted", [128, Q, 8])
            left = sb4("left", [128, Q, W])
            chosen = sb4("chosen", [128, Q, E])
            counts = sb4("counts", [1, XSTEPS * Q * E])
            taken = sb4("taken", [1, XSTEPS, E])
            bits = sb4("bits", [1, XSTEPS, E])
            bit_sum = sb4("bit_sum", [1, XSTEPS])
            picked = sb4("picked", [128, Q, E])
            total = sb4("total", [128, Q])
            total_eps = sb4("total_eps", [128, Q])
            inv = sb4("inv", [128, Q])
            gate = sb4("gate", [128, Q, E])
            gate_t_sb = sb4("gate_t_sb", [E, N, TC])
            tok_ps = ctx.enter_context(nc.psum_tensor("tok_ps", [128, 512], F32))
            gate_ps = ctx.enter_context(nc.psum_tensor("gate_ps", [E, N, TC], F32))
            count_ps = ctx.enter_context(nc.psum_tensor("count_ps", [128, 512], F32))
            count_ready = sem("count_ready")
            weights_high = sem("weights_high")
            x_copied = sem("x_copied")
            x_used = sem("x_used")
            aff_ready = sem("aff_ready")
            dve_step = sem("dve_step")
            gate_ready = sem("gate_ready")
            gate_turned = sem("gate_turned")
            gate_stored = sem("gate_stored")
            gate_out = sem("gate_out")
            counted = sem("counted")
            flagged = sem("flagged")
            block = ctx.enter_context(nc.Block())
            STEPS = TILES // N

            @block.tensor
            def _(pe):
                def logits(i):
                    after(pe, aff_ready, i)
                    for k in range(N):
                        pe.wait_ge(x_copied, i * N + k + 1)
                        for j in range(4):
                            mm = pe.matmul(tok_ps[:, bass.ts(4 * k + j, E)], x_copy[:, k, bass.ts(j, 128)], gw_sb[:, :],
                                           start=True, stop=True, skip_group_check=True)
                        mm.then_inc(x_used, 1)

                def turn_gates(i):
                    pe.wait_ge(gate_ready, i + 1)
                    pe.matmul(count_ps[0:1, 0:Q * E], ones[:, 0:1], chosen[:, :, :].rearrange("p q e -> p (q e)"),
                              start=True, stop=True).then_inc(count_ready, 1)
                    for k in range(N):
                        after(pe, gate_stored, (i - 1) * N + k + 1)
                        for j in range(4):
                            mm = pe.transpose(gate_ps[:, k, bass.ts(j, 128)], gate[:, 4 * k + j, :], eye[:, :])
                        mm.then_inc(gate_turned, 1)

                logits(0)
                logits(1)
                turn_gates(0)
                with pe.Fori(1, STEPS - 1) as i:
                    logits(i + 1)
                    turn_gates(i)
                turn_gates(STEPS - 1)

            @block.scalar
            def _(act):
                def affinities(i):
                    act.wait_ge(x_used, i * N + N)
                    after(act, gate_ready, i)
                    act.activation(aff[:, :, :], tok_ps[:, 0:Q * E].rearrange("p (q e) -> p q e", e=E),
                                   ACT.Sigmoid).then_inc(aff_ready, 1)

                def store_gates(i):
                    after(act, gate_out, i * 16)
                    for k in range(N):
                        act.wait_ge(gate_turned, i * N + k + 1)
                        act.activation(gate_t_sb[:, k, :], gate_ps[:, k, :], ACT.Identity).then_inc(gate_stored, 1)

                def copy_x(i):
                    after(act, x_used, i * N)
                    act.activation(note[:, :], eps[:, :], ACT.Copy)
                    for k in range(N):
                        act.activation(x_copy[:, k, :], xn[:, bass.ds(i * (N * TC) + k * TC, TC)],
                                       ACT.Copy).then_inc(x_copied, 1)

                copy_x(0)
                affinities(0)
                copy_x(1)
                affinities(1)
                copy_x(2)
                store_gates(0)
                with act.Fori(1, STEPS - 2) as i:
                    affinities(i + 1)
                    copy_x(i + 2)
                    store_gates(i)
                affinities(STEPS - 1)
                store_gates(STEPS - 2)
                store_gates(STEPS - 1)

            @block.gpsimd
            def _(pool):
                for e in range(NE):
                    pool.wait_ge(weights_high, e + 1)
                    pool.tensor_tensor(gu_lo[:, e, :], gu_raw[:, e, :], gu_hi[:, e, :].bitcast(F32), ALU.subtract)
                    pool.tensor_tensor(down_lo[:, e, :], down_raw[:, e, :], down_hi[:, e, :].bitcast(F32),
                                       ALU.subtract)

            @block.vector
            def _(dve):
                dve.memset(score[:, :, :], LOWEST)
                dve.memset(wanted[:, :, :], LOWEST).then_inc(dve_step, 1)
                for e in range(NE):
                    dve.tensor_scalar(gu_hi[:, e, :], gu_raw[:, e, :], 1.0, None, ALU.mult)
                    dve.tensor_scalar(down_hi[:, e, :], down_raw[:, e, :], 1.0, None,
                                      ALU.mult).then_inc(weights_high, 1)
                dve.wait_ge(dve_step, 1)
                CH = 8

                def keep_counts(i):
                    dve.wait_ge(count_ready, i + 1)
                    dve.tensor_scalar(counts[:, bass.ds(i * (Q * E), Q * E)],
                                      count_ps[0:1, 0:Q * E], 1.0, None, ALU.mult).then_inc(counted, 1)

                def step(i):
                    base = i * CH + 1
                    dve.wait_ge(aff_ready, i + 1)
                    dve.tensor_tensor(score[:, :, 0:E], aff[:, :, :],
                                      eb_sb[:, :].unsqueeze(1).broadcast_to([128, Q, E]), ALU.add).then_inc(dve_step, 1)
                    dve.wait_ge(dve_step, base + 1)
                    dve.memset(total_eps[:, :], 0.0)
                    for q in range(Q):
                        a = dve.max(top[:, q, :], score[:, q, 0:E])
                    a.then_inc(dve_step, 1)
                    dve.wait_ge(dve_step, base + 2)
                    dve.tensor_copy(wanted[:, :, 0:TOPK], top[:, :, 0:TOPK]).then_inc(dve_step, 1)
                    dve.wait_ge(dve_step, base + 3)
                    dve.memset(inv[:, :], 0.0)
                    for q in range(Q):
                        a = dve.match_replace(left[:, q, :], wanted[:, q, :], score[:, q, :], LOWEST)
                    a.then_inc(dve_step, 1)
                    if not isinstance(i, int) or i > 0:
                        keep_counts(i - 1)
                    dve.wait_ge(dve_step, base + 4)
                    dve.tensor_scalar(chosen[:, :, :], left[:, :, 0:E], LOWEST, None, ALU.is_le)
                    dve.scalar_tensor_tensor(picked[:, :, :], left[:, :, 0:E], LOWEST, aff[:, :, :],
                                             ALU.is_le, ALU.mult).then_inc(dve_step, 1)
                    dve.wait_ge(dve_step, base + 5)
                    dve.tensor_reduce(total[:, :], picked[:, :, :], AX.X, ALU.add).then_inc(dve_step, 1)
                    dve.wait_ge(dve_step, base + 6)
                    dve.tensor_scalar(total_eps[:, :], total[:, :], 1e-9, None, ALU.add).then_inc(dve_step, 1)
                    dve.wait_ge(dve_step, base + 7)
                    dve.reciprocal(inv[:, :], total_eps[:, :]).then_inc(dve_step, 1)
                    dve.wait_ge(dve_step, base + 8)
                    after(dve, gate_turned, i * N)
                    dve.tensor_tensor(gate[:, :, :], picked[:, :, :],
                                      inv[:, :].unsqueeze(2).broadcast_to([128, Q, E]), ALU.mult).then_inc(gate_ready, 1)

                step(0)
                with dve.Fori(1, STEPS) as i:
                    step(i)
                keep_counts(STEPS - 1)
                dve.wait_ge(counted, STEPS)
                dve.tensor_reduce(taken[:, :, :], counts[:, :].rearrange("o (s q e) -> o s e q", q=Q, e=E),
                                  AX.X, ALU.add).then_inc(flagged, 1)
                dve.wait_ge(flagged, 1)
                dve.scalar_tensor_tensor(bits[:, :, :], taken[:, :, :], 0.5,
                                         pow_sb[:, :].unsqueeze(1).broadcast_to([1, XSTEPS, E]),
                                         ALU.is_gt, ALU.mult).then_inc(flagged, 1)
                dve.wait_ge(flagged, 2)
                dve.tensor_reduce(bit_sum[:, :], bits[:, :, :], AX.X, ALU.add).then_inc(flagged, 1)
                dve.wait_ge(flagged, 3)
                dve.tensor_copy(active[:, :], bit_sum[:, :])

            @block.sync
            def _(sp):
                with sp.Fori(0, STEPS) as i:
                    sp.wait_ge(gate_stored, i * N + N)
                    sp.dma_start(gates_dram[bass.ds(i, 1)].rearrange("o e (k c) -> (o e) k c", k=N),
                                 gate_t_sb[:, :, :]).then_inc(gate_out, 16)
                sp.wait_ge(gate_out, STEPS * 16)

        raw.close()

        with ExitStack() as ctx:
            def sb5(name, shape, dt=F32):
                return ctx.enter_context(nc.sbuf_tensor(name, shape, dt))

            def sem(name):
                return ctx.enter_context(nc.semaphore(name))

            f_hi = sb5("f_hi", [D, 2 * XT], F32R)
            f_lo = sb5("f_lo", [D, 2 * XT], F32R)
            gates = sb5("gates", [D, 2 * XT])
            silu = sb5("silu", [D, 2, XC])
            hidden = sb5("hidden", [D, 2, XC])
            hidden_hi = sb5("hidden_hi", [D, XN, XC], F32R)
            hidden_lo = sb5("hidden_lo", [D, XN, XC], F32R)
            before_hi = sb5("before_hi", [D, D], F32R)
            before_lo = sb5("before_lo", [D, D], F32R)
            zeros = sb5("zeros", [D, D], F32R)
            start_note = sb5("start_note", [1, 3])
            g_ps = ctx.enter_context(nc.psum_tensor("g_ps", [D, 2, 512], F32))
            u_ps = ctx.enter_context(nc.psum_tensor("u_ps", [D, 2, 512], F32))
            acc_ps = ctx.enter_context(nc.psum_tensor("acc_ps", [D, XN, 512], F32))
            zeros_ready = sem("zeros_ready")
            tile_high = sem("tile_high")
            tile_split = sem("tile_split")
            gates_in = [sem("gates_in0"), sem("gates_in1")]
            g_ready = sem("g_ready")
            u_ready = sem("u_ready")
            silu_done = sem("silu_done")
            gated = sem("gated")
            gates_free = sem("gates_free")
            hidden_ready = sem("hidden_ready")
            hidden_high = sem("hidden_high")
            hidden_split = sem("hidden_split")
            down_kept = sem("down_kept")
            down_done = sem("down_done")
            stored = sem("stored")
            result_out = sem("result_out")
            block = ctx.enter_context(nc.Block())

            def over_steps(eng, eng_name, shared_unit, routed_unit, counters, closing=lambda i: None):
                used = eng.alloc_register(f"{eng_name}_used")

                def load_used(i):
                    eng.reg_mov(used, eng.value_load(active[0:1, bass.ds(i, 1)], min_val=0, max_val=2 ** E - 1))

                def routed_units(i):
                    for e in range(E, 0, -1):
                        with eng.If(eng.snap(used) >= (1 << (e - 1))):
                            eng.reg_sub(used, used, 1 << (e - 1))
                            routed_unit(i, e)
                            for reg, _, grows in counters:
                                eng.reg_add(reg, reg, grows)

                load_used(0)
                shared_unit(0)
                for reg, grows, _ in counters:
                    if grows:
                        eng.reg_mov(reg, grows)
                routed_units(0)
                closing(0)
                with eng.Fori(1, XSTEPS) as i:
                    load_used(i)
                    shared_unit(i)
                    for reg, grows, _ in counters:
                        if grows:
                            eng.reg_add(reg, reg, grows)
                    routed_units(i)
                    closing(i)

            def for_next_step(eng, i, work, tiles=range(XN)):
                if isinstance(i, int):
                    for s in tiles:
                        work(i + 1, s)
                else:
                    with eng.If(i < XSTEPS - 1):
                        following = nc.s_assert_within(i + 1, 1, XSTEPS - 1, skip_runtime_bounds_check_because="the If above")
                        for s in tiles:
                            work(following, s)

            @block.sync
            def _(sp):
                routed = sp.alloc_register("sp_routed")
                buf = sp.alloc_register("sp_buf")
                sp.reg_mov(routed, 0)
                sp.reg_mov(buf, 0)

                def load_gates(i, e):
                    r, b = sp.snap(routed), sp.snap(buf)
                    sp.wait_ge(gates_free, r + 1)
                    for half in range(2):
                        part = bass.ts(half, XT // 2)
                        sp.wait_ge(gates_in[half], r * 16 + 16)
                        sp.dma_start(gates[:, bass.ds(b + half * (XT // 2), XT // 2)],
                                     gates_dram[bass.ds(i, 1), e - 1, part].partition_broadcast(D)
                                     ).then_inc(gates_in[half], 16)
                    sp.reg_sub(buf, XT, buf)

                over_steps(sp, "sp", lambda i: None, load_gates, [(routed, 0, 1)])

            @block.gpsimd
            def _(pool):
                tiles = pool.alloc_register("pool_tiles")

                def low_columns(i, s):
                    pool.wait_ge(tile_high, i * XN + s + 1)
                    buf = bass.ds((i & 1) * XT + s * XC, XC)
                    pool.tensor_tensor(f_lo[:, buf], xn[:, bass.ds(i * XT + s * XC, XC)], f_hi[:, buf].bitcast(F32),
                                       ALU.subtract).then_inc(tile_split, 1)

                def low_hidden(n, s):
                    pool.wait_ge(hidden_high, n + 1)
                    pool.tensor_tensor(hidden_lo[:, s, :], hidden[:, s % 2, :], hidden_hi[:, s, :].bitcast(F32),
                                       ALU.subtract).then_inc(hidden_split, 1)

                def shared_unit(i):
                    base = 0 if isinstance(i, int) else pool.snap(tiles)
                    for s in range(XN):
                        low_hidden(base + s, s)
                    for_next_step(pool, i, low_columns, (0, 1))

                def routed_unit(i, e):
                    base = pool.snap(tiles)
                    for s in range(XN):
                        low_hidden(base + s, s)

                pool.memset(start_note[:, 0:1], 0.0).then_inc(gates_free, 2)
                pool.memset(start_note[:, 1:2], 0.0).then_inc(gates_in[0], 16)
                pool.memset(start_note[:, 2:3], 0.0).then_inc(gates_in[1], 16)
                for s in range(XN):
                    low_columns(0, s)
                over_steps(pool, "pool", shared_unit, routed_unit, [(tiles, XN, XN)],
                           lambda i: for_next_step(pool, i, low_columns, (2, 3)))

            @block.tensor
            def _(pe):
                tiles = pe.alloc_register("pe_tiles")

                def gate_up(i, n, s, e):
                    par = i & 1
                    if e == 0:
                        pe.wait_ge(tile_split, i * XN + s + 1)
                    cols_ = bass.ds(par * XT + s * XC, XC)
                    hi, lo = f_hi[:, cols_], f_lo[:, cols_]
                    for w, dst, freed, ready in ((0, g_ps, silu_done, g_ready), (D, u_ps, hidden_ready, u_ready)):
                        after(pe, freed, n - 1)
                        out_ = dst[:, s % 2, 0:XC]
                        pe.matmul(out_, gu_hi[:, e, w:w + D], hi, start=True, stop=False)
                        pe.matmul(out_, gu_hi[:, e, w:w + D], lo, start=False, stop=False)
                        pe.matmul(out_, gu_lo[:, e, w:w + D], hi, start=False, stop=True).then_inc(ready, 1)

                def down_product(n, s, w_hi, w_lo, start):
                    pe.wait_ge(hidden_split, n + 1)
                    out_ = acc_ps[:, s, 0:XC]
                    pe.matmul(out_, w_hi, hidden_hi[:, s, :], start=start, stop=False, skip_group_check=True)
                    pe.matmul(out_, w_hi, hidden_lo[:, s, :], start=False, stop=False, skip_group_check=True)
                    pe.matmul(out_, w_lo, hidden_hi[:, s, :], start=False, stop=False,
                              skip_group_check=True).then_inc(down_done, 1)

                def finish(base, s):
                    if s == 1:
                        pe.wait_ge(down_kept, base)
                    down_product(base - XN + s, s, before_hi[:, :], before_lo[:, :], False)

                def unit(i, e):
                    first = isinstance(i, int) and i == 0 and e == 0
                    base = 0 if first else pe.snap(tiles)
                    for s in range(XN):
                        gate_up(i, base + s, s, e)
                        if s < XN - 1 and not first:
                            finish(base, s + 1)
                    if e == 0:
                        after(pe, stored, (i - 1) * XN + 1)
                    down_product(base, 0, down_hi[:, e, :], down_lo[:, e, :], e == 0)
                    if e == 0:
                        if first:
                            pe.wait_ge(zeros_ready, 1)
                        for s in range(1, XN):
                            after(pe, stored, (i - 1) * XN + s + 1)
                            pe.matmul(acc_ps[:, s, 0:XC], zeros[:, :],
                                      f_hi[:, bass.ds((i & 1) * XT + s * XC, XC)],
                                      start=True, stop=False, skip_group_check=True)

                over_steps(pe, "pe", lambda i: unit(i, 0), unit, [(tiles, XN, XN)])
                base = pe.snap(tiles)
                for s in range(1, XN):
                    finish(base, s)

            @block.scalar
            def _(act):
                tiles = act.alloc_register("act_tiles")

                def unit(i, e):
                    first = isinstance(i, int) and i == 0 and e == 0
                    base = 0 if first else act.snap(tiles)
                    for s in range(XN):
                        if s == XN - 1:
                            if not first:
                                act.wait_ge(down_done, base)
                            act.activation(before_hi[:, :], down_hi[:, e, :].bitcast(F32), ACT.Identity)
                            act.activation(before_lo[:, :], down_lo[:, e, :].bitcast(F32),
                                           ACT.Identity).then_inc(down_kept, XN)
                        act.wait_ge(g_ready, base + s + 1)
                        after(act, hidden_ready, base + s - 1)
                        act.activation(silu[:, s % 2, :], g_ps[:, s % 2, 0:XC], ACT.Silu).then_inc(silu_done, 1)
                        if s > 0:
                            if not first:
                                act.wait_ge(down_done, base + s - XN)
                            high_hidden(base + s - 1, s - 1)
                        elif not first:
                            high_hidden(base - 1, XN - 1)
                    if e == 0 and not first:
                        send(i - 1)

                def high_hidden(n, s):
                    act.wait_ge(hidden_ready, n + 1)
                    act.activation(hidden_hi[:, s, :], hidden[:, s % 2, :], ACT.Identity).then_inc(hidden_high, 1)

                def send(i):
                    act.wait_ge(stored, i * XN + XN)
                    cols_ = bass.ds(i * XT, XT)
                    act.dma_start(out[:, cols_], resid[:, cols_]).then_inc(result_out, 16)

                over_steps(act, "act", lambda i: unit(i, 0), unit, [(tiles, XN, XN)])
                high_hidden(act.snap(tiles) - 1, XN - 1)
                send(XSTEPS - 1)
                act.wait_ge(result_out, XSTEPS * 16)

            @block.vector
            def _(dve):
                tiles = dve.alloc_register("dve_tiles")
                routed = dve.alloc_register("dve_routed")
                buf = dve.alloc_register("dve_buf")

                def store(i, s, n):
                    dve.wait_ge(down_done, n + 1)
                    cols_ = bass.ds(i * XT + s * XC, XC)
                    dve.tensor_tensor(resid[:, cols_], resid[:, cols_], acc_ps[:, s, 0:XC], ALU.add).then_inc(stored, 1)

                def make_hidden(n, s):
                    dve.wait_ge(u_ready, n + 1)
                    after(dve, hidden_split, n - 1)
                    dve.tensor_tensor(hidden[:, s % 2, :], silu[:, s % 2, :], u_ps[:, s % 2, 0:XC],
                                      ALU.mult).then_inc(hidden_ready, 1)

                def shared_unit(i):
                    first = isinstance(i, int)
                    base = 0 if first else dve.snap(tiles)
                    for s in range(XN):
                        if not first:
                            store(i - 1, s, base - XN + s)
                        dve.wait_ge(silu_done, base + s + 1)
                        make_hidden(base + s, s)
                    for_next_step(dve, i, high_columns)

                def high_columns(i, s):
                    dve.tensor_scalar(f_hi[:, bass.ds((i & 1) * XT + s * XC, XC)],
                                      xn[:, bass.ds(i * XT + s * XC, XC)], 1.0, None, ALU.mult).then_inc(tile_high, 1)

                def routed_unit(i, e):
                    base = dve.snap(tiles)
                    r = dve.snap(routed)
                    b = dve.snap(buf)
                    for s in range(XN):
                        dve.wait_ge(silu_done, base + s + 1)
                        if s % 2 == 0:
                            dve.wait_ge(gates_in[s // 2], r * 16 + 32)
                        last = s == XN - 1
                        dve.tensor_tensor(silu[:, s % 2, :], silu[:, s % 2, :],
                                          gates[:, bass.ds(b + s * XC, XC)],
                                          ALU.mult).then_inc(gates_free if last else gated, 1)
                        if last:
                            dve.wait_ge(gates_free, r + 3)
                        else:
                            dve.wait_ge(gated, r * (XN - 1) + s + 1)
                        make_hidden(base + s, s)
                    dve.reg_sub(buf, XT, buf)

                dve.tensor_scalar(zeros[:, :], ones[:, :], 0.0, None, ALU.mult).then_inc(zeros_ready, 1)
                for s in range(XN):
                    high_columns(0, s)
                dve.reg_mov(routed, 0)
                dve.reg_mov(buf, 0)
                over_steps(dve, "dve", shared_unit, routed_unit, [(tiles, XN, XN), (routed, 0, 1)])
                base = dve.snap(tiles)
                for s in range(XN):
                    store(XSTEPS - 1, s, base - XN + s)


def kernel(**inputs):
    import numpy as np
    import concourse.bacc as bacc
    from concourse.bass_utils import run_bass_kernel_spmd

    a = {k: np.asarray(v) for k, v in inputs.items()}
    x = a["x"].reshape(B // IMG_LOAD, IMG_LOAD, 3, 11, 16, 13, 16)
    x = x.transpose(0, 4, 6, 2, 1, 3, 5).reshape(B // IMG_LOAD, PK, 128, IMG_LOAD * NP).transpose(0, 2, 1, 3)
    cols = np.concatenate([a["L0_tok_b"][:, None], a["L0_tok_cls_token"].reshape(D, 1), a["L0_attn_bd"][:, None],
                           a["L0_attn_mixing"].T, a["L0_attn_Wb"].T], axis=1)
    gu = np.concatenate([a["L0_ffn_shared_gate_up"][None], a["L0_ffn_expert_gate_up"]], axis=0)
    dn = np.concatenate([a["L0_ffn_shared_down"][None], a["L0_ffn_expert_down"]], axis=0)
    laid = {
        "xp": x,
        "w_tok": a["L0_tok_W"].T.reshape(PK, 128, D),
        "cols": cols,
        "pos": a["L0_tok_pos_emb"].reshape(L),
        "wq": a["L0_attn_Wq"],
        "wk": a["L0_attn_Wk"],
        "wv_t": a["L0_attn_Wv"].T,
        "wd_t": a["L0_attn_Wd"].T,
        "gate_t": a["L0_ffn_gate_w"].T,
        "ebias": a["L0_ffn_expert_bias"],
        "egu_t": gu.transpose(2, 0, 1),
        "ed_t": dn.transpose(2, 0, 1),
        "ident": np.eye(D, dtype=np.float32),
        "centring": np.eye(D, dtype=np.float32) - np.float32(1 / D),
        "powers": (2.0 ** np.arange(E, dtype=np.float32)).reshape(1, E),
    }
    nc = bacc.Bacc("TRN2", target_bir_lowering=False, num_devices=1)
    arrays, args = {}, []
    for name, v in laid.items():
        arrays[name] = np.ascontiguousarray(v)
        args.append(nc.dram_tensor(name, arrays[name].shape, F32, kind="ExternalInput").ap())
    out = nc.dram_tensor("out", (D, T), F32, kind="ExternalOutput").ap()
    tower(nc, *args, out)
    r = run_bass_kernel_spmd(nc, [arrays], core_ids=[0])
    return r.results[0]["out"].reshape(D, B, L).transpose(1, 2, 0)
```
